# Optimizing a Trainium2 kernel written in Bass

```python
import numpy as np
import jax
import jax.numpy as jnp

def _softmax(x, axis=-1):
    return jax.nn.softmax(x, axis=axis)

def _gelu(x):
    return jax.nn.gelu(x, approximate=True)

def _silu(x):
    return jax.nn.silu(x)

def _sigmoid(x):
    return jax.nn.sigmoid(x)

def _layernorm(x, axis=-1, eps=1e-05):
    m = jnp.mean(x, axis=axis, keepdims=True)
    v = jnp.var(x, axis=axis, keepdims=True)
    return (x - m) / jnp.sqrt(v + eps)

def _scatter_add(tgt, idx, src, axis=0):
    return tgt.at[idx].add(src)

def _segment_sum(src, seg, n):
    return jax.ops.segment_sum(src, seg, n)
kernel_name = 'mk_decoder_preln_d1_seqx_r4_e1fce4'

def setup_inputs(seed: int=0):
    np.random.seed(seed)
    _w = jnp.asarray

    def _rec_inputs():
        import jax
        import jax.numpy as jnp
        _rk = jax.random.key(seed)
        x = 7.22e-05 + 1 * jax.random.normal(jax.random.fold_in(_rk, 1), (16, 128, 512), jnp.float32)
        _lenS = 128 - jax.random.randint(jax.random.fold_in(_rk, 7), (16,), 0, max(1, 128 // 4) + 1, jnp.int32)
        _lenS2 = 128 - jax.random.randint(jax.random.fold_in(_rk, 8), (16,), 0, max(1, 128 // 4) + 1, jnp.int32)
        _ctx_512P = jax.random.normal(jax.random.fold_in(_rk, 11), (16, 16, 128), jnp.float32)
        _ctx_512c = jax.random.dirichlet(jax.random.fold_in(_rk, 511), 0.3 * jnp.ones((16,), jnp.float32), (16, 128))
        _ctx_512t = jnp.einsum('bsk,bkd->bsd', _ctx_512c, _ctx_512P)
        _ctx_512t = _ctx_512t * jax.lax.rsqrt(jnp.mean(jnp.square(_ctx_512t)) + 1e-12) * 0.953939
        ctx_512 = -0.000514642 + 1.00011 * (_ctx_512t + 0.3 * jax.random.normal(jax.random.fold_in(_rk, 611), (16, 128, 128), jnp.float32))
        return (x, ctx_512)
    x, ctx_512 = _rec_inputs()

    def _L0_attn_setup():
        import math
        import jax, jax.numpy as jnp
        import numpy as np
        B, S, HID = (4, 256, 512)
        H = 16
        G = 16
        SUBH = H // G
        QDIM = HID // H
        ROPE_THETA = 10000.0

        def rope(t, head_dim=QDIM):
            b, s, hid = t.shape
            t = t.reshape(b, s, hid // head_dim, head_dim)
            half = head_dim // 2
            inv_freq = 1.0 / ROPE_THETA ** (jnp.arange(0, half, dtype=jnp.float32) / half)
            ang = jnp.arange(s, dtype=jnp.float32)[:, None] * inv_freq[None, :]
            cos = jnp.cos(ang)[None, :, None, :]
            sin = jnp.sin(ang)[None, :, None, :]
            t1, t2 = (t[..., :half], t[..., half:])
            out = jnp.concatenate([t1 * cos - t2 * sin, t1 * sin + t2 * cos], axis=-1)
            return out.reshape(b, s, hid)
        key = jax.random.key(seed)
        ks = jax.random.split(key, 9)
        sc = 1.0 / math.sqrt(HID)
        return {'x': jax.random.normal(ks[0], (B, S, HID), dtype=jnp.float32), 'Wq': jax.random.normal(ks[1], (HID, HID), dtype=jnp.float32) * sc, 'bq': jnp.zeros((HID,), dtype=jnp.float32), 'Wk': jax.random.normal(ks[2], (HID, HID), dtype=jnp.float32) * sc, 'bk': jnp.zeros((HID,), dtype=jnp.float32), 'Wv': jax.random.normal(ks[3], (HID, HID), dtype=jnp.float32) * sc, 'bv': jnp.zeros((HID,), dtype=jnp.float32), 'Wo': jax.random.normal(ks[4], (HID, HID), dtype=jnp.float32) * sc, 'bo': jnp.zeros((HID,), dtype=jnp.float32)}
    _L0_attn_all = _L0_attn_setup()
    _L0_attn_in = {k: v for k, v in _L0_attn_all.items() if k in ('Wq', 'bq', 'Wk', 'bk', 'Wv', 'bv', 'Wo', 'bo')}
    del _L0_attn_all

    def _L0_xattn_setup():
        import jax, jax.numpy as jnp
        import numpy as np
        B, S, H, NH, L = (2, 512, 512, 16, 128)
        HD = H // NH
        key = jax.random.key(seed)
        k1, k2, k3, k4, k5 = jax.random.split(key, 5)
        scale = 0.02
        return {'q': jax.random.normal(k1, (B, S, H), dtype=jnp.float32), 'latent_kv': jax.random.normal(k2, (B, S, L), dtype=jnp.float32), 'Wq': jax.random.normal(k3, (H, H), dtype=jnp.float32) * scale, 'Wkv_expand': jax.random.normal(k4, (2 * H, L), dtype=jnp.float32) * scale, 'Wout': jax.random.normal(k5, (H, H), dtype=jnp.float32) * scale}
    _L0_xattn_all = _L0_xattn_setup()
    _L0_xattn_in = {k: v for k, v in _L0_xattn_all.items() if k in ('Wq', 'Wkv_expand', 'Wout')}
    del _L0_xattn_all

    def _L0_ffn_setup():
        import jax, jax.numpy as jnp
        import numpy as np
        TOP_K = 8
        NUM_EXPERTS = 32
        key = jax.random.key(seed)
        k1, k2, k3, k4, k5 = jax.random.split(key, 5)
        B, S, D, M, E = (4, 256, 512, 192, NUM_EXPERTS)
        return {'hidden_states': jax.random.normal(k1, (B, S, D), dtype=jnp.float32), 'gate_kernel': jax.random.normal(k2, (D, E), dtype=jnp.float32) * 0.02, 'gate_proj': jax.random.normal(k3, (E, D, M), dtype=jnp.float32) * 0.02, 'up_proj': jax.random.normal(k4, (E, D, M), dtype=jnp.float32) * 0.02, 'down_proj': jax.random.normal(k5, (E, M, D), dtype=jnp.float32) * 0.02}
    _L0_ffn_all = _L0_ffn_setup()
    _L0_ffn_in = {k: v for k, v in _L0_ffn_all.items() if k in ('gate_kernel', 'gate_proj', 'up_proj', 'down_proj')}
    del _L0_ffn_all
    return {'x': x, 'ctx_512': ctx_512, 'L0_attn_Wq': _L0_attn_in['Wq'], 'L0_attn_bq': _L0_attn_in['bq'], 'L0_attn_Wk': _L0_attn_in['Wk'], 'L0_attn_bk': _L0_attn_in['bk'], 'L0_attn_Wv': _L0_attn_in['Wv'], 'L0_attn_bv': _L0_attn_in['bv'], 'L0_attn_Wo': _L0_attn_in['Wo'], 'L0_attn_bo': _L0_attn_in['bo'], 'L0_xattn_Wq': _L0_xattn_in['Wq'], 'L0_xattn_Wkv_expand': _L0_xattn_in['Wkv_expand'], 'L0_xattn_Wout': _L0_xattn_in['Wout'], 'L0_ffn_gate_kernel': _L0_ffn_in['gate_kernel'], 'L0_ffn_gate_proj': _L0_ffn_in['gate_proj'], 'L0_ffn_up_proj': _L0_ffn_in['up_proj'], 'L0_ffn_down_proj': _L0_ffn_in['down_proj']}

def reference(x, ctx_512, L0_attn_Wq, L0_attn_bq, L0_attn_Wk, L0_attn_bk, L0_attn_Wv, L0_attn_bv, L0_attn_Wo, L0_attn_bo, L0_xattn_Wq, L0_xattn_Wkv_expand, L0_xattn_Wout, L0_ffn_gate_kernel, L0_ffn_gate_proj, L0_ffn_up_proj, L0_ffn_down_proj):
    import jax
    import jax.numpy as jnp

    def _L0_attn_ref(x, Wq, bq, Wk, bk, Wv, bv, Wo, bo):
        import math
        import jax, jax.numpy as jnp
        import numpy as np
        B, S, HID = (4, 256, 512)
        H = 16
        G = 16
        SUBH = H // G
        QDIM = HID // H
        ROPE_THETA = 10000.0

        def rope(t, head_dim=QDIM):
            b, s, hid = t.shape
            t = t.reshape(b, s, hid // head_dim, head_dim)
            half = head_dim // 2
            inv_freq = 1.0 / ROPE_THETA ** (jnp.arange(0, half, dtype=jnp.float32) / half)
            ang = jnp.arange(s, dtype=jnp.float32)[:, None] * inv_freq[None, :]
            cos = jnp.cos(ang)[None, :, None, :]
            sin = jnp.sin(ang)[None, :, None, :]
            t1, t2 = (t[..., :half], t[..., half:])
            out = jnp.concatenate([t1 * cos - t2 * sin, t1 * sin + t2 * cos], axis=-1)
            return out.reshape(b, s, hid)
        b, s, _ = x.shape
        q = x @ Wq.T + bq
        k = x @ Wk.T + bk
        v = x @ Wv.T + bv
        q = rope(q)
        k = rope(k)
        q = q.reshape(b, s, G, SUBH, QDIM).transpose(0, 2, 3, 1, 4)
        k = k.reshape(b, s, G, HID // G).transpose(0, 2, 1, 3)
        v = v.reshape(b, s, G, HID // G).transpose(0, 2, 1, 3)
        scores = jnp.einsum('bgqtd,bgsd->bgqts', q, k) / math.sqrt(QDIM)
        attn = jax.nn.softmax(scores, axis=-1)
        out = jnp.einsum('bgqts,bgsd->bgqtd', attn, v)
        out = out.transpose(0, 3, 1, 2, 4).reshape(b, s, HID)
        return out @ Wo.T + bo

    def _L0_xattn_ref(q, latent_kv, Wq, Wkv_expand, Wout):
        import jax, jax.numpy as jnp
        import numpy as np
        B, S, H, NH, L = (2, 512, 512, 16, 128)
        HD = H // NH
        b, sq, _ = q.shape
        sk = latent_kv.shape[1]
        qp = q @ Wq.T
        kv = latent_kv @ Wkv_expand.T
        k, v = jnp.split(kv, 2, axis=-1)
        qh = qp.reshape(b, sq, NH, HD).transpose(0, 2, 1, 3)
        kh = k.reshape(b, sk, NH, HD).transpose(0, 2, 1, 3)
        vh = v.reshape(b, sk, NH, HD).transpose(0, 2, 1, 3)
        inv_sqrt_d = 1.0 / jnp.sqrt(jnp.float32(HD))
        scores = jnp.einsum('bhqd,bhkd->bhqk', qh, kh) * inv_sqrt_d
        causal = jnp.tril(jnp.ones((sq, sk), dtype=bool))
        scores = jnp.where(causal, scores, jnp.finfo(scores.dtype).min)
        attn = jax.nn.softmax(scores, axis=-1)
        out = jnp.einsum('bhqk,bhkd->bhqd', attn, vh)
        out = out.transpose(0, 2, 1, 3).reshape(b, sq, H)
        return out @ Wout.T

    def _L0_ffn_ref(hidden_states, gate_kernel, gate_proj, up_proj, down_proj):
        import jax, jax.numpy as jnp
        import numpy as np
        TOP_K = 8
        NUM_EXPERTS = 32
        B, S, D = hidden_states.shape
        T = B * S
        x2d = hidden_states.reshape(T, D)
        router_logits = x2d @ gate_kernel
        routing_weights = jax.nn.softmax(router_logits, axis=-1)
        routing_weights, selected_experts = jax.lax.top_k(routing_weights, TOP_K)
        routing_weights = routing_weights / jnp.sum(routing_weights, axis=-1, keepdims=True)
        flat_experts = selected_experts.reshape(-1)
        sort_idx = jnp.argsort(flat_experts)
        token_rows = sort_idx // TOP_K
        sorted_inputs = jnp.take(x2d, token_rows, axis=0)
        group_sizes = jnp.bincount(flat_experts, length=NUM_EXPERTS).astype(jnp.int32)
        w0 = jax.lax.ragged_dot(sorted_inputs, gate_proj, group_sizes, preferred_element_type=jnp.float32)
        w1 = jax.lax.ragged_dot(sorted_inputs, up_proj, group_sizes, preferred_element_type=jnp.float32)
        inter = jax.nn.silu(w0) * w1
        expert_out = jax.lax.ragged_dot(inter, down_proj, group_sizes, preferred_element_type=jnp.float32)
        unsorted = jnp.take(expert_out, jnp.argsort(sort_idx), axis=0)
        per_token = unsorted.reshape(T, TOP_K, D)
        output = jnp.einsum('BKE,BK->BE', per_token.astype(jnp.float32), routing_weights.astype(jnp.float32))
        return output.reshape(B, S, D)
    x = x + _L0_attn_ref(_layernorm(x, axis=-1), L0_attn_Wq, L0_attn_bq, L0_attn_Wk, L0_attn_bk, L0_attn_Wv, L0_attn_bv, L0_attn_Wo, L0_attn_bo)
    x = x + _L0_xattn_ref(_layernorm(x, axis=-1), ctx_512, L0_xattn_Wq, L0_xattn_Wkv_expand, L0_xattn_Wout)
    x = x + _L0_ffn_ref(_layernorm(x, axis=-1), L0_ffn_gate_kernel, L0_ffn_gate_proj, L0_ffn_up_proj, L0_ffn_down_proj)
    return x

_drawn_inputs = setup_inputs


def setup_inputs(seed=0):
    import zlib

    import numpy as np

    out = dict(_drawn_inputs(seed))
    spreads = {'L0_attn_bq': (0.0, 0.573),
     'L0_attn_bk': (0.0, 0.582),
     'L0_attn_bv': (0.0, 0.1),
     'L0_attn_bo': (0.0, 0.1)}
    factors = {'L0_xattn_Wq': 8.0,
     'L0_ffn_gate_kernel': 6.06,
     'L0_ffn_gate_proj': 5.404,
     'L0_ffn_up_proj': 5.274,
     'L0_ffn_down_proj': 5.29}
    for name, (base, spread) in spreads.items():
        noise = np.random.default_rng([zlib.crc32(name.encode()), seed]).standard_normal(out[name].shape)
        drawn = base * np.exp(spread * noise) if base else spread * noise
        out[name] = jnp.asarray(drawn.astype(out[name].dtype))
    for name, factor in factors.items():
        out[name] = (out[name] * factor).astype(out[name].dtype)
    return out
```

```python
from contextlib import ExitStack

import concourse.bass as bass
from concourse import mybir

ALU = mybir.AluOpType
ACT = mybir.ActivationFunctionType
AX_X = mybir.AxisListType.X
F32 = mybir.dt.float32
BF16 = mybir.dt.bfloat16
U32 = mybir.dt.uint32
I32 = mybir.dt.int32

P = 128
SEQS, TOK, D = 16, 128, 512
HEADS, HD = 16, 32
KC = D // P
EXPERTS, TOP_K, MID = 32, 8, 192
TOKENS = SEQS * TOK
TILE = 256
SUBS = TILE // P
LIST_ROWS = EXPERTS * TOKENS + TILE
MOE_TILES = (TOKENS * TOP_K // TILE + EXPERTS - 1 + 1) // 2 * 2
DUMP = TILE
INV_SQRT_HD = float(HD) ** -0.5
EPS = 1e-5
ROUTE_LINKS = 14


def after(eng, sem, count):
    if isinstance(count, int) and count <= 0:
        return
    eng.wait_ge(sem, count)


def apart(eng):
    eng.nop(nofuse=True)


def build(nc, x, ctxT, w_attn, w_kv, w_gate, w_gu, w_dn, biases, ident, identb, rope, causal,
          upper, onesb, iota_e, list_rows0, iota_p, list_fill, out):
    with ExitStack() as ctx:
        def sb(name, shape, dt=F32):
            return ctx.enter_context(nc.sbuf_tensor(name, shape, dt))

        def sem(name):
            return ctx.enter_context(nc.semaphore(name))

        h_dram = nc.dram_tensor("h_rows", (TOKENS + DUMP, D), F32, kind="Internal").ap()
        list_dram = nc.dram_tensor("expert_lists", (LIST_ROWS, 2), U32, kind="Internal").ap()
        tab_dram = nc.dram_tensor("tile_table", (P, 2), I32, kind="Internal").ap()

        S = ctx.enter_context(nc.psum_tensor("scores_ps", [P, 4, 512], F32))
        T = [ctx.enter_context(nc.psum_tensor(f"t{n}_ps", [P, 512], F32)) for n in range(2)]
        A = ctx.enter_context(nc.psum_tensor("a_ps", [P, 512], F32))
        B = ctx.enter_context(nc.psum_tensor("b_ps", [P, 512], F32))

        ident_sb = sb("ident_sb", [P, P])
        identb_sb = sb("identb_sb", [P, P], BF16)
        rope_sb = sb("rope_sb", [P, 2, HD])
        causal_sb = sb("causal_sb", [P, 512], BF16)
        upper_sb = sb("upper_sb", [P, P], BF16)
        onesb_sb = sb("onesb_sb", [P, P], BF16)
        iota_e_sb = sb("iota_e_sb", [P, EXPERTS])
        rows0_sb = sb("rows0_sb", [P, EXPERTS])
        iota_p_sb = sb("iota_p_sb", [P, 1])
        bias_sb = sb("bias_sb", [P, 4, D])
        zeros_sb = sb("zeros_sb", [P, 2 * D])
        half_sb = sb("half_sb", [P, 1])
        x_in = sb("x_in", [P, D])
        resid = sb("resid", [P, D])
        xn = {c: sb(f"xn_{c}", [P, D]) for c in "sxh"}
        xnT = {c: sb(f"xnT_{c}", [P, KC, P]) for c in "sxh"}
        stats = {c: sb(f"stats_{c}", [P, 6]) for c in "sxh"}
        mv = {c: sb(f"mv_{c}", [P, 2]) for c in "sxh"}
        vare = {c: sb(f"vare_{c}", [P, 1]) for c in "sxh"}
        rstd = {c: sb(f"rstd_{c}", [P, 1]) for c in "sxh"}
        qk = sb("qk", [P, 2, D])
        rope_c = sb("rope_c", [P, 2, D])
        rope_s = sb("rope_s", [P, 2, D])
        qk_r = sb("qk_r", [P, 2, D])
        ctx_in = sb("ctx_in", [P, P])
        qT = {c: sb(f"qT_{c}", [P, KC, P]) for c in "sx"}
        kT = {c: sb(f"kT_{c}", [P, KC, P]) for c in "sx"}
        v = {c: sb(f"v_{c}", [P, D]) for c in "sx"}
        nmax = {c: sb(f"nmax_{c}", [P, HEADS]) for c in "sx"}
        rsum = {c: sb(f"rsum_{c}", [P, HEADS]) for c in "sx"}
        rinv = {c: sb(f"rinv_{c}", [P, HEADS]) for c in "sx"}
        probs = {c: sb(f"probs_{c}", [P, HEADS, TOK]) for c in "sx"}
        pT = {c: sb(f"pT_{c}", [P, HEADS, TOK]) for c in "sx"}
        o = {c: sb(f"o_{c}", [P, D]) for c in "sx"}
        oT = {c: sb(f"oT_{c}", [P, KC, P]) for c in "sx"}
        x1 = sb("x1", [P, D])
        x1_held = sb("x1_held", [P, D])
        x2 = sb("x2", [P, D])
        lmax = sb("lmax", [P, 1])
        gate_e = sb("gate_e", [P, EXPERTS])
        top_v = sb("top_v", [P, TOP_K])
        top_i = sb("top_i", [P, TOP_K], U32)
        top_f = sb("top_f", [P, TOP_K])
        top_s = sb("top_s", [P, 1])
        top_r = sb("top_r", [P, 1])
        onehot = sb("onehot", [P, TOP_K, EXPERTS])
        chosen = sb("chosen", [P, EXPERTS], BF16)
        chosen_cum = sb("chosen_cum", [P, EXPERTS], BF16)
        row_of = sb("row_of", [P, EXPERTS])
        row_sel = sb("row_sel", [P, TOP_K, EXPERTS])
        pos_f = sb("pos_f", [P, TOP_K])
        pos_u = sb("pos_u", [P, TOP_K], U32)
        rec = sb("rec", [P, TOP_K, 2], U32)
        tok_f = sb("tok_f", [P, 1])

        def sems(names):
            return {n: sem(n) for n in names.split()}
        g = sems("consts_in w_self_in w_rest_in zeroed dump_out half_set cum_zero "
                 "x_in_s resid_done ctx_in_s q_mm k_mm v_mm kx_mm vx_mm qx_mm qk_done rope_s_done rope_c_done "
                 "rope_done qT_tr kT_tr x1_done held_done x2_done x2_out h_out logits_mm lmax_done ex_done "
                 "route_link rank_mm rec_tok tok_adv list_out")
        xn_done, xnT_tr, xnT_done, stats_done, mv_done, vare_done, rstd_done = (
            {c: sem(f"{n}_{c}") for c in "sxh"} for n in
            ("xn_done", "xnT_tr", "xnT_done", "stats_done", "mv_done", "vare_done", "rstd_done"))
        qT_done, kT_done, v_done, scores_mm, nmax_done, exp_done, pT_tr, pT_act, pT_dve, rinv_done, pv_mm, \
            o_done, oT_tr, oT_done, wo_mm = (
                {c: sem(f"{n}_{c}") for c in "sx"} for n in
                ("qT_done", "kT_done", "v_done", "scores_mm", "nmax_done", "exp_done", "pT_tr", "pT_act",
                 "pT_dve", "rinv_done", "pv_mm", "o_done", "oT_tr", "oT_done", "wo_mm"))
        m = sems("cum_mm tab_link tab_out tab_in w0_in w1_in l0_in l1_in g0_in g1_in xT_mm xT_act xT_dve "
                 "gu_mm silu_done inter_done dn_mm y_act y_dve added")

        steps = [
            -1, 0, 1, 2]
        LOOP = (3, SEQS - 1)
        tail = [SEQS - 1, SEQS, SEQS + 1]

        def run_steps(eng, step):
            for i in steps:
                step(i, i >= 0, i >= 1, i >= 2, True)
            with eng.Fori(*LOOP) as i:
                step(i, True, True, True, True)
            for i in tail:
                step(i, i < SEQS, i <= SEQS, True, False)

        with ExitStack() as wctx:
            def wsb(name, shape, dt=F32):
                return wctx.enter_context(nc.sbuf_tensor(name, shape, dt))
            w_sb = wsb("w_sb", [P, 6, KC, D])
            w_kv_sb = wsb("w_kv_sb", [P, 2 * D])
            w_gate_sb = wsb("w_gate_sb", [P, KC, EXPERTS])

            block = wctx.enter_context(nc.Block())

            @block.sync
            def _(sp):
                for dst, src in ((ident_sb, ident), (identb_sb, identb), (rope_sb, rope), (causal_sb, causal),
                                 (upper_sb, upper), (onesb_sb, onesb), (iota_e_sb, iota_e),
                                 (rows0_sb, list_rows0), (iota_p_sb, iota_p), (bias_sb, biases)):
                    sp.dma_start(dst[:], src).then_inc(g["consts_in"], 16)

                def step(i, own, cross, route, ahead):
                    if ahead:
                        after(sp, xn_done["s"], i + 1)
                        after(sp, g["resid_done"], i + 1)
                        sp.dma_start(x_in[:], x[i + 1] if isinstance(i, int)
                                     else x[bass.ds(i + 1, 1)].rearrange("a t d -> (a t) d")
                                     ).then_inc(g["x_in_s"], 16)
                    if isinstance(i, int) and i == -1:
                        for n in range(3):
                            sp.dma_start(w_sb[:, n], w_attn[:, n]).then_inc(g["w_self_in"], 16)
                        for n in range(3, 6):
                            sp.dma_start(w_sb[:, n], w_attn[:, n]).then_inc(g["w_rest_in"], 16)
                        sp.dma_start(w_kv_sb[:], w_kv).then_inc(g["w_rest_in"], 16)
                        sp.dma_start(w_gate_sb[:], w_gate).then_inc(g["w_rest_in"], 16)
                        sp.dma_start(list_dram.rearrange("(a b) c -> a (b c)", a=P),
                                     list_fill).then_inc(g["dump_out"], 16)
                        sp.wait_ge(g["zeroed"], 1)
                        for t in (h_dram, out):
                            sp.dma_start(t[TOKENS:].rearrange("(p s) d -> p (s d)", p=P),
                                         zeros_sb[:]).then_inc(g["dump_out"], 16)
                    if own:
                        after(sp, g["vx_mm"], i)
                        sp.dma_start(ctx_in[:], ctxT[i] if isinstance(i, int)
                                     else ctxT[bass.ds(i, 1)].rearrange("a t d -> (a t) d")
                                     ).then_inc(g["ctx_in_s"], 16)
                    if cross:
                        rows = slice((i - 1) * P, i * P) if isinstance(i, int) else bass.ds((i - 1) * P, P)
                        sp.wait_ge(g["x2_done"], i)
                        sp.dma_start(out[rows, :], x2[:]).then_inc(g["x2_out"], 16)
                        sp.wait_ge(xn_done["h"], i)
                        sp.dma_start(h_dram[rows, :], xn["h"][:]).then_inc(g["h_out"], 16)

                run_steps(sp, step)

            @block.tensor
            def _(pe):
                def transposes(dst, src, done):
                    for c in range(KC):
                        mm = nc.tensor.transpose(dst[:, c * P:(c + 1) * P], src[:, c * P:(c + 1) * P], ident_sb[:])
                    mm.then_inc(done, 1)

                def project(dst, lhsT, w, done):
                    for c in range(KC):
                        mm = nc.tensor.matmul(dst[:], lhsT[:, c], w[:, c], start=(c == 0), stop=(c == KC - 1))
                    mm.then_inc(done, 1)

                def scores(c):
                    masked = c == "x"
                    if masked:
                        for r in range(4):
                            nc.tensor.matmul(S[:, r], identb_sb[:], causal_sb[:], start=True, stop=False,
                                             skip_group_check=True)
                    for k in range(KC):
                        for r in range(4):
                            rows = slice(HD * r, HD * (r + 1))
                            mm = nc.tensor.matmul(S[:, r, k * TOK:(k + 1) * TOK], qT[c][rows, k], kT[c][rows, k],
                                                  start=not masked, stop=True, skip_group_check=True)
                    mm.then_inc(scores_mm[c], 1)

                def probs_T(c, j):
                    for r in range(4):
                        pe.wait_ge(exp_done[c], HEADS * j + 4 * (r + 1))
                        if r >= 2:
                            pe.wait_ge((pT_act if r == 2 else pT_dve)[c], 2 * j + 1)
                        for k in range(KC):
                            mm = nc.tensor.transpose(T[r % 2][:, k * P:(k + 1) * P], probs[c][:, 4 * r + k], ident_sb[:])
                        mm.then_inc(pT_tr[c], 1)

                def weighted_v(c, j, dst):
                    pe.wait_ge(pT_act[c], 2 * (j + 1))
                    pe.wait_ge(pT_dve[c], 2 * (j + 1))
                    for k in range(KC):
                        for r in range(4):
                            h = 4 * k + r
                            mm = nc.tensor.matmul(dst[:, h * HD:(h + 1) * HD], pT[c][:, 4 * r + k],
                                                  v[c][:, h * HD:(h + 1) * HD], start=True, stop=True)
                    mm.then_inc(pv_mm[c], 1)

                pe.wait_ge(g["consts_in"], 16 * 10)

                def step(i, own, cross, route, ahead):
                    first = isinstance(i, int)
                    if own:
                        pe.wait_ge(qT_done["s"], i + 1)
                        pe.wait_ge(kT_done["s"], i + 1)
                        after(pe, exp_done["x"], HEADS * (i - 1))
                        scores("s")
                    if route:
                        pe.wait_ge(xn_done["h"], i - 1)
                        transposes(T[0], xn["h"], xnT_tr["h"])
                    if cross:
                        if first and i == 1:
                            pe.wait_ge(g["w_rest_in"], 16 * 5)
                        pe.wait_ge(g["ctx_in_s"], 16 * i)
                        pe.wait_ge(g["x1_done"], i)
                        for c in range(KC):
                            mm = nc.tensor.matmul(A[:, c * P:(c + 1) * P], w_kv_sb[:, c * P:(c + 1) * P], ctx_in[:],
                                                  start=True, stop=True)
                        mm.then_inc(g["kx_mm"], 1)
                        after(pe, g["route_link"], ROUTE_LINKS * (i - 2))
                        nc.tensor.matmul(B[:], ctx_in[:], w_kv_sb[:, D:], start=True, stop=True
                                         ).then_inc(g["vx_mm"], 1)
                    if route:
                        pe.wait_ge(xnT_done["h"], i - 1)
                        for c in range(KC):
                            mm = nc.tensor.matmul(T[1][:, 0:EXPERTS], xnT["h"][:, c], w_gate_sb[:, c],
                                                  start=(c == 0), stop=(c == KC - 1))
                        mm.then_inc(g["logits_mm"], 1)
                    if cross:
                        pe.wait_ge(xn_done["x"], i)
                        transposes(T[0], xn["x"], xnT_tr["x"])
                        pe.wait_ge(xnT_done["x"], i)
                        pe.wait_ge(kT_done["x"], i)
                        for f in range(KC):
                            for c in range(KC):
                                mm = nc.tensor.matmul(A[:, f * P:(f + 1) * P], w_sb[:, 4, c, f * P:(f + 1) * P],
                                                      xnT["x"][:, c], start=(c == 0), stop=(c == KC - 1))
                        mm.then_inc(g["qx_mm"], 1)
                    if own:
                        if route:
                            pe.wait_ge(g["ex_done"], i - 1)
                        pe.wait_ge(v_done["s"], i + 1)
                        probs_T("s", i)
                        if cross:
                            pe.wait_ge(qT_done["x"], i)
                            pe.wait_ge(v_done["x"], i)
                        weighted_v("s", i, A)
                        pe.wait_ge(o_done["s"], i + 1)
                        transposes(B, o["s"], oT_tr["s"])
                        if first and i == 0:
                            pe.wait_ge(g["w_rest_in"], 16 * 5)
                        pe.wait_ge(oT_done["s"], i + 1)
                        project(A, oT["s"], w_sb[:, 3], wo_mm["s"])
                    if route:
                        if cross and not own:
                            pe.wait_ge(v_done["x"], i)
                        pe.wait_ge(g["route_link"], ROUTE_LINKS * (i - 2) + 8)
                        nc.tensor.matmul(B[:, 0:EXPERTS], upper_sb[:], chosen[:], start=True, stop=False)
                        nc.tensor.matmul(B[:, 0:EXPERTS], onesb_sb[:], chosen_cum[:], start=False, stop=True
                                         ).then_inc(g["rank_mm"], 1)
                    if cross:
                        pe.wait_ge(qT_done["x"], i)
                        if own:
                            pe.wait_ge(exp_done["s"], HEADS * (i + 1))
                        scores("x")
                    if ahead:
                        if first and i == -1:
                            pe.wait_ge(g["w_self_in"], 16 * 3)
                        pe.wait_ge(xn_done["s"], i + 2)
                        transposes(T[0], xn["s"], xnT_tr["s"])
                        pe.wait_ge(xnT_done["s"], i + 2)
                        after(pe, g["x1_done"], i + 1)
                        project(A, xnT["s"], w_sb[:, 0], g["q_mm"])
                        if route:
                            pe.wait_ge(g["route_link"], ROUTE_LINKS * (i - 2) + 10)
                        project(B, xnT["s"], w_sb[:, 1], g["k_mm"])
                        project(T[1], xnT["s"], w_sb[:, 2], g["v_mm"])
                    if cross:
                        if ahead:
                            pe.wait_ge(v_done["s"], i + 2)
                        elif route:
                            pe.wait_ge(g["ex_done"], i - 1)
                        probs_T("x", i - 1)
                        weighted_v("x", i - 1, T[0])
                    if ahead:
                        pe.wait_ge(g["rope_done"], i + 2)
                        transposes(A, qk_r[:, 0], g["qT_tr"])
                        transposes(B, qk_r[:, 1], g["kT_tr"])
                    if cross:
                        pe.wait_ge(o_done["x"], i)
                        transposes(T[1], o["x"], oT_tr["x"])
                        pe.wait_ge(oT_done["x"], i)
                        project(T[0], oT["x"], w_sb[:, 5], wo_mm["x"])

                run_steps(pe, step)

            @block.scalar
            def _(act):
                def exps(c, j):
                    after(act, pT_tr[c], 4 * j)
                    after(act, rinv_done[c], j)
                    act.wait_ge(nmax_done[c], j + 1)
                    for r in range(4):
                        for k in range(KC):
                            n = 4 * r + k
                            nc.scalar.activation(probs[c][:, n], S[:, r, k * TOK:(k + 1) * TOK], ACT.Exp,
                                                 bias=nmax[c][:, n:n + 1],
                                                 accum_out=rsum[c][:, n:n + 1]).then_inc(exp_done[c], 1)

                def pT_half(c, j):
                    after(act, pv_mm[c], j)
                    for r in (0, 2):
                        act.wait_ge(pT_tr[c], 4 * j + r + 1)
                        nc.scalar.copy(pT[c][:, 4 * r:4 * r + 4].rearrange("p h t -> p (h t)"), T[0][:]
                                       ).then_inc(pT_act[c], 1)

                def oT_copy(c, j, src):
                    act.wait_ge(oT_tr[c], j + 1)
                    after(act, wo_mm[c], j)
                    nc.scalar.copy(oT[c][:].rearrange("p k t -> p (k t)"), src[:]).then_inc(oT_done[c], 1)

                def step(i, own, cross, route, ahead):
                    if own:
                        exps("s", i)
                    if route:
                        act.wait_ge(g["lmax_done"], i - 1)
                        after(act, g["route_link"], ROUTE_LINKS * (i - 3) + 2)
                        nc.scalar.activation(gate_e[:], T[1][:, 0:EXPERTS], ACT.Exp, bias=lmax[:]
                                             ).then_inc(g["ex_done"], 1)
                    if own:
                        pT_half("s", i)
                        oT_copy("s", i, B)
                    if cross:
                        exps("x", i - 1)
                        pT_half("x", i - 1)
                    if ahead:
                        act.wait_ge(g["qT_tr"], i + 2)
                        after(act, scores_mm["s"], i + 1)
                        nc.scalar.mul(qT["s"][:].rearrange("p k t -> p (k t)"), A[:], INV_SQRT_HD
                                      ).then_inc(qT_done["s"], 1)
                    if cross:
                        oT_copy("x", i - 1, T[1])

                run_steps(act, step)

            @block.vector
            def _(dve):
                def flat(t):
                    return t[:].rearrange("p k t -> p (k t)")

                def norm_stats(c, j, src):
                    nc.vector.bn_stats(stats[c][:], src[:]).then_inc(stats_done[c], 1)
                    dve.wait_ge(stats_done[c], j + 1)
                    apart(dve)
                    nc.vector.bn_aggr(mv[c][:], stats[c][:]).then_inc(mv_done[c], 1)

                def normalise(c, j, src):
                    dve.wait_ge(rstd_done[c], j + 1)
                    nc.vector.tensor_scalar(xn[c][:], src[:], mv[c][:, 0:1], rstd[c][:], ALU.subtract,
                                            ALU.mult).then_inc(xn_done[c], 1)

                def row_max(c, j):
                    dve.wait_ge(scores_mm[c], j + 1)
                    after(dve, exp_done[c], HEADS * j)
                    nc.vector.tensor_reduce(nmax[c][:], S[:].rearrange("p r (k t) -> p (r k) t", k=KC), AX_X,
                                            ALU.max, negate=True).then_inc(nmax_done[c], 1)

                def invert_sums(c, j):
                    dve.wait_ge(exp_done[c], HEADS * (j + 1))
                    nc.vector.reciprocal(rinv[c][:], rsum[c][:]).then_inc(rinv_done[c], 1)

                def pT_half(c, j):
                    after(dve, pv_mm[c], j)
                    for r in (1, 3):
                        dve.wait_ge(pT_tr[c], 4 * j + r + 1)
                        nc.vector.tensor_copy(pT[c][:, 4 * r:4 * r + 4].rearrange("p h t -> p (h t)"), T[1][:]
                                              ).then_inc(pT_dve[c], 1)

                def scale_out(c, j, src):
                    dve.wait_ge(pv_mm[c], j + 1)
                    dve.wait_ge(rinv_done[c], j + 1)
                    after(dve, oT_tr[c], j)
                    nc.vector.tensor_tensor(
                        o[c][:].rearrange("p (k r d) -> p k r d", k=KC, r=4),
                        src[:].rearrange("p (k r d) -> p k r d", k=KC, r=4),
                        rinv[c][:].rearrange("p (r k) -> p k r", r=4).unsqueeze(3).to_broadcast([P, KC, 4, HD]),
                        ALU.mult).then_inc(o_done[c], 1)

                def link(j, n, ins):
                    ins.then_inc(g["route_link"], 1)
                    dve.wait_ge(g["route_link"], ROUTE_LINKS * j + n)

                nc.vector.memset(zeros_sb[:], 0.0).then_inc(g["zeroed"], 1)
                nc.vector.memset(chosen_cum[:], 0.0).then_inc(g["cum_zero"], 1)
                dve.wait_ge(g["consts_in"], 16 * 10)

                def step(i, own, cross, route, ahead):
                    if own:
                        row_max("s", i)
                    if route:
                        dve.wait_ge(xnT_tr["h"], i - 1)
                        after(dve, g["logits_mm"], i - 2)
                        nc.vector.tensor_copy(flat(xnT["h"]), T[0][:]).then_inc(xnT_done["h"], 1)
                    if cross:
                        dve.wait_ge(g["kx_mm"], i)
                        after(dve, scores_mm["x"], i - 1)
                        nc.vector.tensor_copy(flat(kT["x"]), A[:]).then_inc(kT_done["x"], 1)
                        dve.wait_ge(g["vx_mm"], i)
                        after(dve, pv_mm["x"], i - 1)
                        nc.vector.tensor_copy(v["x"][:], B[:]).then_inc(v_done["x"], 1)
                    if route:
                        dve.wait_ge(g["logits_mm"], i - 1)
                        after(dve, g["ex_done"], i - 2)
                        nc.vector.tensor_reduce(lmax[:], T[1][:, 0:EXPERTS], AX_X, ALU.max, negate=True
                                                ).then_inc(g["lmax_done"], 1)
                    if cross:
                        dve.wait_ge(xnT_tr["x"], i)
                        after(dve, g["qx_mm"], i - 1)
                        nc.vector.tensor_copy(flat(xnT["x"]), T[0][:]).then_inc(xnT_done["x"], 1)
                        dve.wait_ge(g["qx_mm"], i)
                        nc.vector.tensor_scalar(flat(qT["x"]), A[:], INV_SQRT_HD, None, ALU.mult
                                                ).then_inc(qT_done["x"], 1)
                    if own:
                        pT_half("s", i)
                        invert_sums("s", i)
                        scale_out("s", i, A)
                    if route:
                        j = i - 2
                        dve.wait_ge(g["ex_done"], i - 1)
                        after(dve, g["list_out"], 16 * TOP_K * (i - 2))
                        apart(dve)
                        link(j, 1, nc.vector.max(top_v[:], gate_e[:]))
                        apart(dve)
                        link(j, 2, nc.vector.max_index(top_i[:], top_v[:], gate_e[:]))
                        link(j, 3, nc.vector.tensor_reduce(top_s[:], top_v[:], AX_X, ALU.add))
                        link(j, 4, nc.vector.reciprocal(top_r[:], top_s[:]))
                        link(j, 5, nc.vector.tensor_scalar(rec[:].bitcast(F32)[:, :, 1], top_v[:], top_r[:], None,
                                                           ALU.mult))
                        link(j, 6, nc.vector.tensor_copy(top_f[:], top_i[:]))
                        link(j, 7, nc.vector.tensor_tensor(
                            onehot[:], iota_e_sb[:].unsqueeze(1).to_broadcast([P, TOP_K, EXPERTS]),
                            top_f[:].unsqueeze(2).to_broadcast([P, TOP_K, EXPERTS]), ALU.is_equal))
                        with nc.allow_low_precision(reason="sums of zeros and ones are exact"):
                            link(j, 8, nc.vector.tensor_reduce(chosen[:], onehot[:].rearrange("p k e -> p e k"),
                                                               AX_X, ALU.add))
                    if own:
                        dve.wait_ge(wo_mm["s"], i + 1)
                        dve.wait_ge(g["resid_done"], i + 1)
                        after(dve, g["held_done"], i)
                        nc.vector.tensor_tensor(x1[:], A[:], resid[:], ALU.add).then_inc(g["x1_done"], 1)
                        dve.wait_ge(g["x1_done"], i + 1)
                        norm_stats("x", i, x1)
                    if ahead:
                        dve.wait_ge(g["x_in_s"], 16 * (i + 2))
                        norm_stats("s", i + 1, x_in)
                    if own:
                        after(dve, xnT_tr["x"], i)
                        normalise("x", i, x1)
                    if ahead:
                        after(dve, xnT_tr["s"], i + 1)
                        normalise("s", i + 1, x_in)
                    if route:
                        dve.wait_ge(g["rank_mm"], i - 1)
                        link(j, 9, nc.vector.tensor_tensor(chosen_cum[:], chosen_cum[:], chosen[:], ALU.add))
                        link(j, 10, nc.vector.tensor_tensor(row_of[:], B[:, 0:EXPERTS], rows0_sb[:], ALU.add))
                        link(j, 11, nc.vector.tensor_tensor(
                            row_sel[:], onehot[:], row_of[:].unsqueeze(1).to_broadcast([P, TOP_K, EXPERTS]),
                            ALU.mult))
                        link(j, 12, nc.vector.tensor_reduce(pos_f[:], row_sel[:], AX_X, ALU.add))
                        link(j, 13, nc.vector.tensor_copy(pos_u[:], pos_f[:]))
                        link(j, 14, nc.vector.tensor_copy(top_s[:], top_r[:]))
                    if cross:
                        row_max("x", i - 1)
                    if ahead:
                        dve.wait_ge(xnT_tr["s"], i + 2)
                        after(dve, g["v_mm"], i + 1)
                        nc.vector.tensor_copy(flat(xnT["s"]), T[0][:]).then_inc(xnT_done["s"], 1)
                        after(dve, g["rope_s_done"], 2 * (i + 1))
                        dve.wait_ge(g["q_mm"], i + 2)
                        nc.vector.tensor_tensor(qk[:, 0], A[:], bias_sb[:, 0], ALU.add).then_inc(g["qk_done"], 1)
                        dve.wait_ge(g["k_mm"], i + 2)
                        nc.vector.tensor_tensor(qk[:, 1], B[:], bias_sb[:, 1], ALU.add).then_inc(g["qk_done"], 1)
                        dve.wait_ge(g["qk_done"], 2 * (i + 2))
                        nc.vector.tensor_tensor(
                            rope_c[:].rearrange("p a (h d) -> p (a h) d", d=HD),
                            qk[:].rearrange("p a (h d) -> p (a h) d", d=HD),
                            rope_sb[:, 0].unsqueeze(1).to_broadcast([P, 2 * HEADS, HD]), ALU.mult
                        ).then_inc(g["rope_c_done"], 1)
                        dve.wait_ge(g["v_mm"], i + 2)
                        after(dve, pv_mm["s"], i + 1)
                        nc.vector.tensor_tensor(v["s"][:], T[1][:], bias_sb[:, 2], ALU.add).then_inc(v_done["s"], 1)
                        dve.wait_ge(g["rope_c_done"], i + 2)
                        dve.wait_ge(g["rope_s_done"], 2 * (i + 2))
                        after(dve, g["kT_tr"], i + 1)
                        nc.vector.tensor_tensor(qk_r[:], rope_c[:], rope_s[:], ALU.add).then_inc(g["rope_done"], 1)
                    if cross:
                        pT_half("x", i - 1)
                        invert_sums("x", i - 1)
                        scale_out("x", i - 1, T[0])
                    if ahead:
                        dve.wait_ge(g["kT_tr"], i + 2)
                        after(dve, scores_mm["s"], i + 1)
                        nc.vector.tensor_copy(flat(kT["s"]), B[:]).then_inc(kT_done["s"], 1)
                    if cross:
                        dve.wait_ge(wo_mm["x"], i)
                        dve.wait_ge(g["held_done"], i)
                        after(dve, g["x2_out"], 16 * (i - 1))
                        nc.vector.tensor_tensor(x2[:], T[0][:], x1_held[:], ALU.add).then_inc(g["x2_done"], 1)
                        dve.wait_ge(g["x2_done"], i)
                        norm_stats("h", i - 1, x2)
                        after(dve, xnT_tr["h"], i - 1)
                        after(dve, g["h_out"], 16 * (i - 1))
                        normalise("h", i - 1, x2)

                run_steps(dve, step)

            @block.gpsimd
            def _(pool):
                nc.gpsimd.memset(half_sb[:], -0.5).then_inc(g["half_set"], 1)
                pool.wait_ge(g["half_set"], 1)
                pool.wait_ge(g["consts_in"], 16 * 10)
                nc.gpsimd.tensor_copy(tok_f[:], iota_p_sb[:]).then_inc(g["tok_adv"], 1)
                pool.wait_ge(g["dump_out"], 16 * 3)

                def inv_std(c, j):
                    pool.wait_ge(mv_done[c], j + 1)
                    apart(pool)
                    nc.gpsimd.tensor_scalar(vare[c][:], mv[c][:, 1:2], EPS, None, ALU.add).then_inc(vare_done[c], 1)
                    pool.wait_ge(vare_done[c], j + 1)
                    nc.gpsimd.tensor_tensor(rstd[c][:], vare[c][:], half_sb[:], ALU.pow).then_inc(rstd_done[c], 1)

                def step(i, own, cross, route, ahead):
                    if own:
                        inv_std("x", i)
                    if ahead:
                        inv_std("s", i + 1)
                        pool.wait_ge(g["x_in_s"], 16 * (i + 2))
                        after(pool, g["x1_done"], i + 1)
                        nc.gpsimd.tensor_tensor(resid[:], x_in[:], bias_sb[:, 3], ALU.add
                                                ).then_inc(g["resid_done"], 1)
                        after(pool, g["rope_done"], i + 1)
                        pool.wait_ge(g["qk_done"], 2 * (i + 2))
                        src = qk[:].rearrange("p a (h s d) -> p (a h) s d", s=2, d=HD // 2)
                        dst = rope_s[:].rearrange("p a (h s d) -> p (a h) s d", s=2, d=HD // 2)
                        sin = rope_sb[:, 1].rearrange("p (s d) -> p s d", s=2)
                        for s in range(2):
                            nc.gpsimd.tensor_tensor(
                                dst[:, :, s], src[:, :, 1 - s],
                                sin[:, s].unsqueeze(1).to_broadcast([P, 2 * HEADS, HD // 2]), ALU.mult
                            ).then_inc(g["rope_s_done"], 1)
                    if route:
                        j = i - 2
                        after(pool, g["list_out"], 16 * TOP_K * (i - 2))
                        pool.wait_ge(g["tok_adv"], i - 1)
                        apart(pool)
                        nc.gpsimd.tensor_copy(rec[:, :, 0], tok_f[:].to_broadcast([P, TOP_K])
                                              ).then_inc(g["rec_tok"], 1)
                        pool.wait_ge(g["rec_tok"], i - 1)
                        apart(pool)
                        nc.gpsimd.tensor_scalar(tok_f[:], tok_f[:], float(TOK), None, ALU.add
                                                ).then_inc(g["tok_adv"], 1)
                        pool.wait_ge(g["route_link"], ROUTE_LINKS * j + 13)
                        apart(pool)
                        for k in range(TOP_K):
                            pool.indirect_dma_start(
                                out=list_dram[:, :], out_offset=bass.IndirectOffsetOnAxis(ap=pos_u[:, k:k + 1], axis=0),
                                in_=rec[:, k, :], in_offset=None).then_inc(g["list_out"], 16)
                    if cross:
                        inv_std("h", i - 1)
                    if own:
                        pool.wait_ge(g["x1_done"], i + 1)
                        after(pool, g["x2_done"], i)
                        apart(pool)
                        nc.gpsimd.tensor_copy(x1_held[:], x1[:]).then_inc(g["held_done"], 1)

                run_steps(pool, step)

        cnt = sb("cnt", [P, EXPERTS])
        cnt_i = sb("cnt_i", [P, EXPERTS], I32)
        cnt_s = sb("cnt_s", [P, EXPERTS], I32)
        ntile = sb("ntile", [P, EXPERTS])
        ncum = sb("ncum", [P, EXPERTS])
        passed = sb("passed", [P, EXPERTS])
        passed_n = sb("passed_n", [P, EXPERTS])
        tab_e = sb("tab_e", [P, 1])
        tab_a = sb("tab_a", [P, 1])
        tab_b = sb("tab_b", [P, 1])
        tab_c = sb("tab_c", [P, 1])
        tab = sb("tab", [P, 2], I32)
        tab_row = sb("tab_row", [1, 2 * P], I32)
        gu_sb = sb("gu_sb", [P, 2, KC, 2 * MID])
        dn_a = sb("dn_a", [P, 2, D])
        dn_b = sb("dn_b", [P, 2, D])
        lst = sb("lst", [P, 2, SUBS, 2], U32)
        xg = sb("xg", [P, 2, SUBS, D])
        xgT = sb("xgT", [P, 2, KC, TILE])
        silu_a = sb("silu_a", [P, TILE])
        silu_b = sb("silu_b", [P, TILE])
        int_a = sb("int_a", [P, TILE])
        int_b = sb("int_b", [P, TILE])
        y = sb("y", [P, 2, SUBS, D])
        lst_f = lst[:].bitcast(F32)
        MA = P
        MB = MID - P

        block2 = ctx.enter_context(nc.Block())
        PAIRS = MOE_TILES // 2

        @block2.sync
        def _(sp):
            sp.wait_ge(m["tab_link"], 13)
            sp.dma_start(tab_dram, tab[:]).then_inc(m["tab_out"], 16)
            sp.wait_ge(m["tab_out"], 16)
            sp.dma_start(tab_row[:], tab_dram.rearrange("(o p) c -> o (p c)", o=1)).then_inc(m["tab_in"], 16)
            sp.wait_ge(m["tab_in"], 16)
            sp.wait_ge(g["list_out"], 16 * TOP_K * SEQS)

            def load(t, s, waits):
                e = sp.value_load(tab_row[0:1, bass.ds(2 * t, 1)], min_val=0, max_val=EXPERTS - 1)
                r = sp.value_load(tab_row[0:1, bass.ds(2 * t + 1, 1)], min_val=0, max_val=LIST_ROWS - TILE)
                if waits:
                    sp.wait_ge(m["added"], 16 * SUBS * (t - 1))
                sp.dma_start(lst[:, s], list_dram[bass.ds(r, TILE), :].rearrange("(s p) c -> p s c", s=SUBS)
                             ).then_inc(m[f"l{s}_in"], 16)
                if waits:
                    sp.wait_ge(m["dn_mm"], SUBS * (t - 1))
                sp.dma_start(gu_sb[:, s], w_gu[bass.ds(e, 1)].rearrange("a p k n -> (a p) k n")
                             ).then_inc(m[f"w{s}_in"], 16)
                sp.dma_start(dn_a[:, s], w_dn[bass.ds(e, 1), 0:MA].rearrange("a p n -> (a p) n")
                             ).then_inc(m[f"w{s}_in"], 16)
                sp.dma_start(dn_b[0:MB, s], w_dn[bass.ds(e, 1), MA:MID].rearrange("a p n -> (a p) n")
                             ).then_inc(m[f"w{s}_in"], 16)

            for s in range(2):
                load(s, s, False)
            with sp.Fori(1, PAIRS) as i:
                for s in range(2):
                    load(2 * i + s, s, True)
            sp.wait_ge(m["added"], 16 * SUBS * MOE_TILES)
            sp.wait_ge(g["x2_out"], 16 * SEQS)
            sp.wait_ge(g["h_out"], 16 * SEQS)

        @block2.gpsimd
        def _(pool):
            pool.wait_ge(g["h_out"], 16 * SEQS)
            pool.wait_ge(g["x2_out"], 16 * SEQS)

            def gather(t, s, n, waits):
                if waits:
                    pool.wait_ge(m["xT_mm"], 2 * (t - 1))
                pool.wait_ge(m[f"l{s}_in"], 16 * n)
                apart(pool)
                for q in range(SUBS):
                    pool.indirect_dma_start(
                        out=xg[:, s, q], out_offset=None, in_=h_dram[:, :],
                        in_offset=bass.IndirectOffsetOnAxis(ap=lst[:, s, q, 0:1], axis=0)
                    ).then_inc(m[f"g{s}_in"], 16)

            def add(t, s, last):
                if last:
                    pool.wait_ge(m["added"], 16 * SUBS * t)
                pool.wait_ge(m["y_act"], t + 1)
                pool.wait_ge(m["y_dve"], t + 1)
                apart(pool)
                for q in range(SUBS):
                    pool.indirect_dma_start(
                        out=out[:, :], out_offset=bass.IndirectOffsetOnAxis(ap=lst[:, s, q, 0:1], axis=0),
                        in_=y[:, s, q], in_offset=None, compute_op=ALU.add).then_inc(m["added"], 16)

            gather(0, 0, 1, False)
            gather(1, 1, 1, False)
            add(0, 0, False)
            with pool.Fori(1, PAIRS) as i:
                gather(2 * i, 0, i + 1, True)
                add(2 * i - 1, 1, True)
                gather(2 * i + 1, 1, i + 1, True)
                add(2 * i, 0, True)
            add(MOE_TILES - 1, 1, True)

        @block2.tensor
        def _(pe):
            pe.wait_ge(g["route_link"], ROUTE_LINKS * SEQS)
            nc.tensor.matmul(A[:, 0:EXPERTS], onesb_sb[:], chosen_cum[:], start=True, stop=True
                             ).then_inc(m["cum_mm"], 1)

            def turn(t, s, n, waits):
                pe.wait_ge(m[f"g{s}_in"], 16 * SUBS * n)
                if waits:
                    pe.wait_ge(m["xT_act"], t)
                    pe.wait_ge(m["xT_dve"], t)
                for k in range(KC):
                    for q in range(SUBS):
                        mm = nc.tensor.transpose(S[:, k // 2, (k % 2) * TILE + q * P:(k % 2) * TILE + (q + 1) * P],
                                                 xg[:, s, q, k * P:(k + 1) * P], ident_sb[:])
                    if k % 2:
                        mm.then_inc(m["xT_mm"], 1)

            def gate_up(t, s, n, waits):
                pe.wait_ge(m["xT_act"], t + 1)
                pe.wait_ge(m["xT_dve"], t + 1)
                pe.wait_ge(m[f"w{s}_in"], 48 * n)
                if waits:
                    pe.wait_ge(m["inter_done"], 2 * t)
                for c, dst in ((0, S[:, 2, 0:TILE]), (1, S[:, 2, TILE:2 * TILE]), (2, S[:, 3, 0:TILE])):
                    for k in range(KC):
                        mm = nc.tensor.matmul(dst, gu_sb[:, s, k, c * P:(c + 1) * P], xgT[:, s, k],
                                              start=(k == 0), stop=(k == KC - 1))
                    if c:
                        mm.then_inc(m["gu_mm"], 1)

            def down(t, s, waits):
                pe.wait_ge(m["inter_done"], 2 * (t + 1))
                if waits:
                    pe.wait_ge(m["y_act"], t)
                    pe.wait_ge(m["y_dve"], t)
                for q in range(SUBS):
                    nc.tensor.matmul(T[q][:], int_a[:, q * P:(q + 1) * P], dn_a[:, s], start=True, stop=False)
                    nc.tensor.matmul(T[q][:], int_b[0:MB, q * P:(q + 1) * P], dn_b[0:MB, s],
                                     start=False, stop=True).then_inc(m["dn_mm"], 1)

            turn(0, 0, 1, False)
            gate_up(0, 0, 1, False)
            turn(1, 1, 1, True)
            down(0, 0, False)
            with pe.Fori(1, PAIRS) as i:
                gate_up(2 * i - 1, 1, i, True)
                turn(2 * i, 0, i + 1, True)
                down(2 * i - 1, 1, True)
                gate_up(2 * i, 0, i + 1, True)
                turn(2 * i + 1, 1, i + 1, True)
                down(2 * i, 0, True)
            gate_up(MOE_TILES - 1, 1, PAIRS, True)
            down(MOE_TILES - 1, 1, True)

        @block2.scalar
        def _(act):
            def xT_copy(t, s, waits):
                act.wait_ge(m["xT_mm"], 2 * t + 1)
                if waits:
                    act.wait_ge(m["gu_mm"], 2 * (t - 1))
                nc.scalar.copy(xgT[:, s, 0:2].rearrange("p k t -> p (k t)"), S[:, 0]).then_inc(m["xT_act"], 1)

            def silu(t):
                for c, dst, src in ((1, silu_a[:], S[:, 2, 0:TILE]), (2, silu_b[0:MB], S[0:MB, 3, 0:TILE])):
                    act.wait_ge(m["gu_mm"], 2 * t + c)
                    after(act, m["inter_done"], 2 * (t - 1) + c)
                    nc.scalar.activation(dst, src, ACT.Silu).then_inc(m["silu_done"], 1)

            def weigh(t, s, waits):
                act.wait_ge(m["dn_mm"], 2 * t + 1)
                if waits:
                    act.wait_ge(m["added"], 16 * SUBS * (t - 1))
                nc.scalar.activation(y[:, s, 0], T[0][:], ACT.Copy, scale=lst_f[:, s, 0, 1:2]
                                     ).then_inc(m["y_act"], 1)

            xT_copy(0, 0, False)
            silu(0)
            xT_copy(1, 1, False)
            weigh(0, 0, False)
            silu(1)
            xT_copy(2, 0, True)
            weigh(1, 1, False)
            silu(2)
            xT_copy(3, 1, True)
            weigh(2, 0, True)
            with act.Fori(2, PAIRS) as i:
                silu(2 * i - 1)
                xT_copy(2 * i, 0, True)
                weigh(2 * i - 1, 1, True)
                silu(2 * i)
                xT_copy(2 * i + 1, 1, True)
                weigh(2 * i, 0, True)
            silu(MOE_TILES - 1)
            weigh(MOE_TILES - 1, 1, True)

        @block2.vector
        def _(dve):
            def link(n, ins):
                ins.then_inc(m["tab_link"], 1)
                dve.wait_ge(m["tab_link"], n)

            dve.wait_ge(m["cum_mm"], 1)
            link(1, nc.vector.tensor_scalar(cnt[:], A[:, 0:EXPERTS], float(TILE - 1), None, ALU.add))
            link(2, nc.vector.tensor_copy(cnt_i[:], cnt[:]))
            link(3, nc.vector.tensor_scalar(cnt_s[:], cnt_i[:], TILE.bit_length() - 1, None,
                                            ALU.arith_shift_right))
            link(4, nc.vector.tensor_copy(ntile[:], cnt_s[:]))
            link(5, nc.vector.tensor_tensor_scan(ncum[:], zeros_sb[:, 0:EXPERTS], ntile[:], 0.0, ALU.add, ALU.add))
            link(6, nc.vector.tensor_scalar(passed[:], ncum[:], iota_p_sb[:], None, ALU.is_le))
            link(7, nc.vector.tensor_tensor(passed_n[:], passed[:], ntile[:], ALU.mult))
            link(8, nc.vector.tensor_reduce(tab_e[:], passed[:], AX_X, ALU.add))
            link(9, nc.vector.tensor_reduce(tab_a[:], passed_n[:], AX_X, ALU.add))
            link(10, nc.vector.tensor_scalar(tab_b[:], tab_a[:], iota_p_sb[:], -float(TILE), ALU.subtract, ALU.mult))
            link(11, nc.vector.scalar_tensor_tensor(tab_c[:], tab_e[:], float(TOKENS), tab_b[:], ALU.mult, ALU.add))
            link(12, nc.vector.tensor_scalar(tab[:, 1:2], tab_c[:], float(EXPERTS * TOKENS), None, ALU.min))
            link(13, nc.vector.tensor_scalar(tab[:, 0:1], tab_e[:], float(EXPERTS - 1), None, ALU.min))

            def xT_copy(t, s, waits):
                dve.wait_ge(m["xT_mm"], 2 * t + 2)
                if waits:
                    dve.wait_ge(m["gu_mm"], 2 * (t - 1))
                nc.vector.tensor_copy(xgT[:, s, 2:4].rearrange("p k t -> p (k t)"), S[:, 1]
                                      ).then_inc(m["xT_dve"], 1)

            def inter(t):
                if not (isinstance(t, int) and t == 0):
                    dve.wait_ge(m["dn_mm"], 2 * t)
                dve.wait_ge(m["silu_done"], 2 * t + 1)
                nc.vector.tensor_tensor(int_a[:], S[:, 2, TILE:2 * TILE], silu_a[:], ALU.mult
                                        ).then_inc(m["inter_done"], 1)
                dve.wait_ge(m["silu_done"], 2 * t + 2)
                nc.vector.tensor_tensor(int_b[0:MB], S[MB:2 * MB, 3, 0:TILE], silu_b[0:MB], ALU.mult
                                        ).then_inc(m["inter_done"], 1)

            def weigh(t, s, waits):
                dve.wait_ge(m["dn_mm"], 2 * t + 2)
                if waits:
                    dve.wait_ge(m["added"], 16 * SUBS * (t - 1))
                nc.vector.tensor_scalar(y[:, s, 1], T[1][:], lst_f[:, s, 1, 1:2], None, ALU.mult
                                        ).then_inc(m["y_dve"], 1)

            xT_copy(0, 0, False)
            inter(0)
            xT_copy(1, 1, False)
            weigh(0, 0, False)
            inter(1)
            xT_copy(2, 0, True)
            weigh(1, 1, False)
            inter(2)
            xT_copy(3, 1, True)
            weigh(2, 0, True)
            with dve.Fori(2, PAIRS) as i:
                inter(2 * i - 1)
                xT_copy(2 * i, 0, True)
                weigh(2 * i - 1, 1, True)
                inter(2 * i)
                xT_copy(2 * i + 1, 1, True)
                weigh(2 * i, 0, True)
            inter(MOE_TILES - 1)
            weigh(MOE_TILES - 1, 1, True)


def kernel(**inputs):
    import ml_dtypes
    import numpy as np
    import concourse.bacc as bacc
    from concourse.bass_utils import run_bass_kernel_spmd

    a = {k: np.ascontiguousarray(np.asarray(v)) for k, v in inputs.items()}

    def by_rows(w):
        return w.reshape(w.shape[0] // P, P, w.shape[1]).transpose(1, 0, 2)

    w_attn = np.stack([by_rows(a[n].T) for n in ("L0_attn_Wq", "L0_attn_Wk", "L0_attn_Wv", "L0_attn_Wo",
                                                 "L0_xattn_Wq", "L0_xattn_Wout")], axis=1)
    gate, up = a["L0_ffn_gate_proj"], a["L0_ffn_up_proj"]
    gu = np.concatenate([gate[:, :, :P], up[:, :, :P], gate[:, :, P:], up[:, :, P:]], axis=2)
    gu = gu.reshape(EXPERTS, KC, P, 2 * MID).transpose(0, 2, 1, 3)
    biases = np.broadcast_to(np.stack([a[n] for n in ("L0_attn_bq", "L0_attn_bk", "L0_attn_bv", "L0_attn_bo")]),
                             (P, 4, D))
    half = HD // 2
    freq = (1.0 / 10000.0 ** (np.arange(half, dtype=np.float32) / np.float32(half))).astype(np.float32)
    ang = np.arange(TOK, dtype=np.float32)[:, None] * freq[None, :]
    cos, sin = np.cos(ang), np.sin(ang)
    rope = np.stack([np.concatenate([cos, cos], 1), np.concatenate([-sin, sin], 1)], axis=1)
    t = np.arange(P)
    causal = np.tile(np.where(t[None, :] > t[:, None], -1e30, 0.0), (1, 4))
    fill = np.zeros((LIST_ROWS, 2), np.uint32)
    fill[:, 0] = TOKENS + np.arange(LIST_ROWS) % DUMP
    arrays = {
        "x": a["x"], "ctxT": a["ctx_512"].transpose(0, 2, 1), "w_attn": w_attn,
        "w_kv": a["L0_xattn_Wkv_expand"].T, "w_gate": by_rows(a["L0_ffn_gate_kernel"]),
        "w_gu": gu, "w_dn": a["L0_ffn_down_proj"], "biases": biases,
        "ident": np.eye(P, dtype=np.float32), "identb": np.eye(P).astype(ml_dtypes.bfloat16),
        "rope": rope.astype(np.float32), "causal": causal.astype(ml_dtypes.bfloat16),
        "upper": (t[:, None] < t[None, :]).astype(ml_dtypes.bfloat16),
        "onesb": np.ones((P, P), ml_dtypes.bfloat16),
        "iota_e": np.broadcast_to(np.arange(EXPERTS, dtype=np.float32), (P, EXPERTS)),
        "list_rows0": np.broadcast_to(np.arange(EXPERTS, dtype=np.float32) * TOKENS, (P, EXPERTS)),
        "iota_p": t[:, None].astype(np.float32), "list_fill": fill.reshape(P, -1),
    }
    arrays = {k: np.ascontiguousarray(v) for k, v in arrays.items()}
    nc = bacc.Bacc("TRN2", target_bir_lowering=False, num_devices=1)
    args = [nc.dram_tensor(k, v.shape, mybir.dt.from_np(v.dtype), kind="ExternalInput").ap()
            for k, v in arrays.items()]
    out = nc.dram_tensor("out_rows", (TOKENS + DUMP, D), F32, kind="ExternalOutput").ap()
    build(nc, *args, out)
    r = run_bass_kernel_spmd(nc, [arrays], core_ids=[0])
    return r.results[0]["out_rows"][:TOKENS].reshape(SEQS, TOK, D)
```

```python
from contextlib import ExitStack

import concourse.bass as bass
from concourse import mybir

ALU = mybir.AluOpType
ACT = mybir.ActivationFunctionType
AX_X = mybir.AxisListType.X
F32 = mybir.dt.float32
BF16 = mybir.dt.bfloat16
F16 = mybir.dt.float16
U32 = mybir.dt.uint32
I32 = mybir.dt.int32

P = 128
SEQS, TOK, D = 16, 128, 512
HEADS, HD = 16, 32
KC = D // P
EXPERTS, TOP_K, MID = 32, 8, 192
TOKENS = SEQS * TOK
TILE = 256
SUBS = TILE // P
LIST_ROWS = EXPERTS * TOKENS + TILE
RING = 8
MOE_TILES = -(-(TOKENS * TOP_K // TILE + EXPERTS - 1) // RING) * RING
LIST_AHEAD, ROW_AHEAD, SPLIT_AHEAD = 6, 4, 3
MB = MID - P
WA = KC * 2 * MID + D
W_SCALE = 64.0
DUMP = TILE
INV_SQRT_HD = float(HD) ** -0.5
EPS = 1e-5
ROUTE_LINKS = 14


def after(eng, sem, count):
    if isinstance(count, int) and count <= 0:
        return
    eng.wait_ge(sem, count)


def apart(eng):
    eng.nop(nofuse=True)


def build(nc, x, ctxT, w_attn, w_kv, w_gate, w_a, w_b, biases, ident, identb, rope, causal,
          upper, onesb, iota_e, list_rows0, iota_p, list_fill, out):
    with ExitStack() as ctx:
        def sb(name, shape, dt=F32):
            return ctx.enter_context(nc.sbuf_tensor(name, shape, dt))

        def sem(name):
            return ctx.enter_context(nc.semaphore(name))

        h_dram = nc.dram_tensor("h_rows", (TOKENS + DUMP, D), F32, kind="Internal").ap()
        list_dram = nc.dram_tensor("expert_lists", (LIST_ROWS, 2), U32, kind="Internal").ap()
        tab_dram = nc.dram_tensor("tile_table", (P, 2), I32, kind="Internal").ap()

        S = ctx.enter_context(nc.psum_tensor("scores_ps", [P, 4, 512], F32))
        T = [ctx.enter_context(nc.psum_tensor(f"t{n}_ps", [P, 512], F32)) for n in range(2)]
        A = ctx.enter_context(nc.psum_tensor("a_ps", [P, 512], F32))
        B = ctx.enter_context(nc.psum_tensor("b_ps", [P, 512], F32))

        ident_sb = sb("ident_sb", [P, P])
        identb_sb = sb("identb_sb", [P, P], BF16)
        rope_sb = sb("rope_sb", [P, 2, HD])
        causal_sb = sb("causal_sb", [P, 512], BF16)
        upper_sb = sb("upper_sb", [P, P], BF16)
        onesb_sb = sb("onesb_sb", [P, P], BF16)
        iota_e_sb = sb("iota_e_sb", [P, EXPERTS])
        rows0_sb = sb("rows0_sb", [P, EXPERTS])
        iota_p_sb = sb("iota_p_sb", [P, 1])
        bias_sb = sb("bias_sb", [P, 4, D])
        zeros_sb = sb("zeros_sb", [P, 2 * D])
        chosen_cum = sb("chosen_cum", [P, EXPERTS], BF16)
        half_sb = sb("half_sb", [P, 1])
        def sems(names):
            return {n: sem(n) for n in names.split()}
        g = sems("consts_in w_self_in w_rest_in zeroed dump_out half_set cum_zero "
                 "x_in_s resid_done ctx_in_s q_mm k_mm v_mm kx_mm vx_mm qx_mm qk_done rope_s_done rope_c_done "
                 "rope_done qT_tr kT_tr x1_done held_done x2_done x2_out h_out logits_mm lmax_done ex_done "
                 "route_link rank_mm rec_tok tok_adv list_out")
        xn_done, xnT_tr, xnT_done, stats_done, mv_done, vare_done, rstd_done = (
            {c: sem(f"{n}_{c}") for c in "sxh"} for n in
            ("xn_done", "xnT_tr", "xnT_done", "stats_done", "mv_done", "vare_done", "rstd_done"))
        qT_done, kT_done, v_done, scores_mm, nmax_done, exp_done, pT_tr, pT_act, pT_dve, rinv_done, pv_mm, \
            o_done, oT_tr, oT_done, wo_mm = (
                {c: sem(f"{n}_{c}") for c in "sx"} for n in
                ("qT_done", "kT_done", "v_done", "scores_mm", "nmax_done", "exp_done", "pT_tr", "pT_act",
                 "pT_dve", "rinv_done", "pv_mm", "o_done", "oT_tr", "oT_done", "wo_mm"))
        m = sems("cum_mm tab_link tab_out tab_in w0_in w1_in l0_in l1_in l2_in l3_in l4_in l5_in l6_in l7_in g0_in g1_in g2_in g3_in "
                 "wa_hi_done wa_lo_done wb_hi_done wb_lo_done xT_mm xT_hi_done xT_lo_done gu_mm silu_done "
                 "mid_done mid_hi_done mid_lo_done dn_mm y_act y_dve added")

        steps = [
            -1, 0, 1, 2]
        LOOP = (3, SEQS - 1)
        tail = [SEQS - 1, SEQS, SEQS + 1]

        def run_steps(eng, step):
            for i in steps:
                step(i, i >= 0, i >= 1, i >= 2, True)
            with eng.Fori(*LOOP) as i:
                step(i, True, True, True, True)
            for i in tail:
                step(i, i < SEQS, i <= SEQS, True, False)

        with ExitStack() as wctx:
            def wsb(name, shape, dt=F32):
                return wctx.enter_context(nc.sbuf_tensor(name, shape, dt))
            w_sb = wsb("w_sb", [P, 6, KC, D])
            w_kv_sb = wsb("w_kv_sb", [P, 2 * D])
            w_gate_sb = wsb("w_gate_sb", [P, KC, EXPERTS])
            x_in = wsb("x_in", [P, D])
            resid = wsb("resid", [P, D])
            xn = {c: wsb(f"xn_{c}", [P, D]) for c in "sxh"}
            xnT = {c: wsb(f"xnT_{c}", [P, KC, P]) for c in "sxh"}
            stats = {c: wsb(f"stats_{c}", [P, 6]) for c in "sxh"}
            mv = {c: wsb(f"mv_{c}", [P, 2]) for c in "sxh"}
            vare = {c: wsb(f"vare_{c}", [P, 1]) for c in "sxh"}
            rstd = {c: wsb(f"rstd_{c}", [P, 1]) for c in "sxh"}
            qk = wsb("qk", [P, 2, D])
            rope_c = wsb("rope_c", [P, 2, D])
            rope_s = wsb("rope_s", [P, 2, D])
            qk_r = wsb("qk_r", [P, 2, D])
            ctx_in = wsb("ctx_in", [P, P])
            qT = {c: wsb(f"qT_{c}", [P, KC, P]) for c in "sx"}
            kT = {c: wsb(f"kT_{c}", [P, KC, P]) for c in "sx"}
            v = {c: wsb(f"v_{c}", [P, D]) for c in "sx"}
            nmax = {c: wsb(f"nmax_{c}", [P, HEADS]) for c in "sx"}
            rsum = {c: wsb(f"rsum_{c}", [P, HEADS]) for c in "sx"}
            rinv = {c: wsb(f"rinv_{c}", [P, HEADS]) for c in "sx"}
            probs = {c: wsb(f"probs_{c}", [P, HEADS, TOK]) for c in "sx"}
            pT = {c: wsb(f"pT_{c}", [P, HEADS, TOK]) for c in "sx"}
            o = {c: wsb(f"o_{c}", [P, D]) for c in "sx"}
            oT = {c: wsb(f"oT_{c}", [P, KC, P]) for c in "sx"}
            x1 = wsb("x1", [P, D])
            x1_held = wsb("x1_held", [P, D])
            x2 = wsb("x2", [P, D])
            lmax = wsb("lmax", [P, 1])
            gate_e = wsb("gate_e", [P, EXPERTS])
            top_v = wsb("top_v", [P, TOP_K])
            top_i = wsb("top_i", [P, TOP_K], U32)
            top_f = wsb("top_f", [P, TOP_K])
            top_s = wsb("top_s", [P, 1])
            top_r = wsb("top_r", [P, 1])
            onehot = wsb("onehot", [P, TOP_K, EXPERTS])
            chosen = wsb("chosen", [P, EXPERTS], BF16)
            row_of = wsb("row_of", [P, EXPERTS])
            row_sel = wsb("row_sel", [P, TOP_K, EXPERTS])
            pos_f = wsb("pos_f", [P, TOP_K])
            pos_u = wsb("pos_u", [P, TOP_K], U32)
            rec = wsb("rec", [P, TOP_K, 2], U32)
            tok_f = wsb("tok_f", [P, 1])

            block = wctx.enter_context(nc.Block())

            @block.sync
            def _(sp):
                for dst, src in ((ident_sb, ident), (identb_sb, identb), (rope_sb, rope), (causal_sb, causal),
                                 (upper_sb, upper), (onesb_sb, onesb), (iota_e_sb, iota_e),
                                 (rows0_sb, list_rows0), (iota_p_sb, iota_p), (bias_sb, biases)):
                    sp.dma_start(dst[:], src).then_inc(g["consts_in"], 16)

                def step(i, own, cross, route, ahead):
                    if ahead:
                        after(sp, xn_done["s"], i + 1)
                        after(sp, g["resid_done"], i + 1)
                        sp.dma_start(x_in[:], x[i + 1] if isinstance(i, int)
                                     else x[bass.ds(i + 1, 1)].rearrange("a t d -> (a t) d")
                                     ).then_inc(g["x_in_s"], 16)
                    if isinstance(i, int) and i == -1:
                        for n in range(3):
                            sp.dma_start(w_sb[:, n], w_attn[:, n]).then_inc(g["w_self_in"], 16)
                        for n in range(3, 6):
                            sp.dma_start(w_sb[:, n], w_attn[:, n]).then_inc(g["w_rest_in"], 16)
                        sp.dma_start(w_kv_sb[:], w_kv).then_inc(g["w_rest_in"], 16)
                        sp.dma_start(w_gate_sb[:], w_gate).then_inc(g["w_rest_in"], 16)
                        sp.dma_start(list_dram.rearrange("(a b) c -> a (b c)", a=P),
                                     list_fill).then_inc(g["dump_out"], 16)
                        sp.wait_ge(g["zeroed"], 1)
                        for t in (h_dram, out):
                            sp.dma_start(t[TOKENS:].rearrange("(p s) d -> p (s d)", p=P),
                                         zeros_sb[:]).then_inc(g["dump_out"], 16)
                    if own:
                        after(sp, g["vx_mm"], i)
                        sp.dma_start(ctx_in[:], ctxT[i] if isinstance(i, int)
                                     else ctxT[bass.ds(i, 1)].rearrange("a t d -> (a t) d")
                                     ).then_inc(g["ctx_in_s"], 16)
                    if cross:
                        rows = slice((i - 1) * P, i * P) if isinstance(i, int) else bass.ds((i - 1) * P, P)
                        sp.wait_ge(g["x2_done"], i)
                        sp.dma_start(out[rows, :], x2[:]).then_inc(g["x2_out"], 16)
                        sp.wait_ge(xn_done["h"], i)
                        sp.dma_start(h_dram[rows, :], xn["h"][:]).then_inc(g["h_out"], 16)

                run_steps(sp, step)

            @block.tensor
            def _(pe):
                def transposes(dst, src, done):
                    for c in range(KC):
                        mm = nc.tensor.transpose(dst[:, c * P:(c + 1) * P], src[:, c * P:(c + 1) * P], ident_sb[:])
                    mm.then_inc(done, 1)

                def project(dst, lhsT, w, done):
                    for c in range(KC):
                        mm = nc.tensor.matmul(dst[:], lhsT[:, c], w[:, c], start=(c == 0), stop=(c == KC - 1))
                    mm.then_inc(done, 1)

                def scores(c):
                    masked = c == "x"
                    if masked:
                        for r in range(4):
                            nc.tensor.matmul(S[:, r], identb_sb[:], causal_sb[:], start=True, stop=False,
                                             skip_group_check=True)
                    for k in range(KC):
                        for r in range(4):
                            rows = slice(HD * r, HD * (r + 1))
                            mm = nc.tensor.matmul(S[:, r, k * TOK:(k + 1) * TOK], qT[c][rows, k], kT[c][rows, k],
                                                  start=not masked, stop=True, skip_group_check=True)
                    mm.then_inc(scores_mm[c], 1)

                def probs_T(c, j):
                    for r in range(4):
                        pe.wait_ge(exp_done[c], HEADS * j + 4 * (r + 1))
                        if r >= 2:
                            pe.wait_ge((pT_act if r == 2 else pT_dve)[c], 2 * j + 1)
                        for k in range(KC):
                            mm = nc.tensor.transpose(T[r % 2][:, k * P:(k + 1) * P], probs[c][:, 4 * r + k], ident_sb[:])
                        mm.then_inc(pT_tr[c], 1)

                def weighted_v(c, j, dst):
                    pe.wait_ge(pT_act[c], 2 * (j + 1))
                    pe.wait_ge(pT_dve[c], 2 * (j + 1))
                    for k in range(KC):
                        for r in range(4):
                            h = 4 * k + r
                            mm = nc.tensor.matmul(dst[:, h * HD:(h + 1) * HD], pT[c][:, 4 * r + k],
                                                  v[c][:, h * HD:(h + 1) * HD], start=True, stop=True)
                    mm.then_inc(pv_mm[c], 1)

                pe.wait_ge(g["consts_in"], 16 * 10)

                def step(i, own, cross, route, ahead):
                    first = isinstance(i, int)
                    if own:
                        pe.wait_ge(qT_done["s"], i + 1)
                        pe.wait_ge(kT_done["s"], i + 1)
                        after(pe, exp_done["x"], HEADS * (i - 1))
                        scores("s")
                    if route:
                        pe.wait_ge(xn_done["h"], i - 1)
                        transposes(T[0], xn["h"], xnT_tr["h"])
                    if cross:
                        if first and i == 1:
                            pe.wait_ge(g["w_rest_in"], 16 * 5)
                        pe.wait_ge(g["ctx_in_s"], 16 * i)
                        pe.wait_ge(g["x1_done"], i)
                        for c in range(KC):
                            mm = nc.tensor.matmul(A[:, c * P:(c + 1) * P], w_kv_sb[:, c * P:(c + 1) * P], ctx_in[:],
                                                  start=True, stop=True)
                        mm.then_inc(g["kx_mm"], 1)
                        after(pe, g["route_link"], ROUTE_LINKS * (i - 2))
                        nc.tensor.matmul(B[:], ctx_in[:], w_kv_sb[:, D:], start=True, stop=True
                                         ).then_inc(g["vx_mm"], 1)
                    if route:
                        pe.wait_ge(xnT_done["h"], i - 1)
                        for c in range(KC):
                            mm = nc.tensor.matmul(T[1][:, 0:EXPERTS], xnT["h"][:, c], w_gate_sb[:, c],
                                                  start=(c == 0), stop=(c == KC - 1))
                        mm.then_inc(g["logits_mm"], 1)
                    if cross:
                        pe.wait_ge(xn_done["x"], i)
                        transposes(T[0], xn["x"], xnT_tr["x"])
                        pe.wait_ge(xnT_done["x"], i)
                        pe.wait_ge(kT_done["x"], i)
                        for f in range(KC):
                            for c in range(KC):
                                mm = nc.tensor.matmul(A[:, f * P:(f + 1) * P], w_sb[:, 4, c, f * P:(f + 1) * P],
                                                      xnT["x"][:, c], start=(c == 0), stop=(c == KC - 1))
                        mm.then_inc(g["qx_mm"], 1)
                    if own:
                        if route:
                            pe.wait_ge(g["ex_done"], i - 1)
                        pe.wait_ge(v_done["s"], i + 1)
                        probs_T("s", i)
                        if cross:
                            pe.wait_ge(qT_done["x"], i)
                            pe.wait_ge(v_done["x"], i)
                        weighted_v("s", i, A)
                        pe.wait_ge(o_done["s"], i + 1)
                        transposes(B, o["s"], oT_tr["s"])
                        if first and i == 0:
                            pe.wait_ge(g["w_rest_in"], 16 * 5)
                        pe.wait_ge(oT_done["s"], i + 1)
                        project(A, oT["s"], w_sb[:, 3], wo_mm["s"])
                    if route:
                        if cross and not own:
                            pe.wait_ge(v_done["x"], i)
                        pe.wait_ge(g["route_link"], ROUTE_LINKS * (i - 2) + 8)
                        nc.tensor.matmul(B[:, 0:EXPERTS], upper_sb[:], chosen[:], start=True, stop=False)
                        nc.tensor.matmul(B[:, 0:EXPERTS], onesb_sb[:], chosen_cum[:], start=False, stop=True
                                         ).then_inc(g["rank_mm"], 1)
                    if cross:
                        pe.wait_ge(qT_done["x"], i)
                        if own:
                            pe.wait_ge(exp_done["s"], HEADS * (i + 1))
                        scores("x")
                    if ahead:
                        if first and i == -1:
                            pe.wait_ge(g["w_self_in"], 16 * 3)
                        pe.wait_ge(xn_done["s"], i + 2)
                        transposes(T[0], xn["s"], xnT_tr["s"])
                        pe.wait_ge(xnT_done["s"], i + 2)
                        after(pe, g["x1_done"], i + 1)
                        project(A, xnT["s"], w_sb[:, 0], g["q_mm"])
                        if route:
                            pe.wait_ge(g["route_link"], ROUTE_LINKS * (i - 2) + 10)
                        project(B, xnT["s"], w_sb[:, 1], g["k_mm"])
                        project(T[1], xnT["s"], w_sb[:, 2], g["v_mm"])
                    if cross:
                        if ahead:
                            pe.wait_ge(v_done["s"], i + 2)
                        elif route:
                            pe.wait_ge(g["ex_done"], i - 1)
                        probs_T("x", i - 1)
                        weighted_v("x", i - 1, T[0])
                    if ahead:
                        pe.wait_ge(g["rope_done"], i + 2)
                        transposes(A, qk_r[:, 0], g["qT_tr"])
                        transposes(B, qk_r[:, 1], g["kT_tr"])
                    if cross:
                        pe.wait_ge(o_done["x"], i)
                        transposes(T[1], o["x"], oT_tr["x"])
                        pe.wait_ge(oT_done["x"], i)
                        project(T[0], oT["x"], w_sb[:, 5], wo_mm["x"])

                run_steps(pe, step)

            @block.scalar
            def _(act):
                def exps(c, j):
                    after(act, pT_tr[c], 4 * j)
                    after(act, rinv_done[c], j)
                    act.wait_ge(nmax_done[c], j + 1)
                    for r in range(4):
                        for k in range(KC):
                            n = 4 * r + k
                            nc.scalar.activation(probs[c][:, n], S[:, r, k * TOK:(k + 1) * TOK], ACT.Exp,
                                                 bias=nmax[c][:, n:n + 1],
                                                 accum_out=rsum[c][:, n:n + 1]).then_inc(exp_done[c], 1)

                def pT_half(c, j):
                    after(act, pv_mm[c], j)
                    for r in (0, 2):
                        act.wait_ge(pT_tr[c], 4 * j + r + 1)
                        nc.scalar.copy(pT[c][:, 4 * r:4 * r + 4].rearrange("p h t -> p (h t)"), T[0][:]
                                       ).then_inc(pT_act[c], 1)

                def oT_copy(c, j, src):
                    act.wait_ge(oT_tr[c], j + 1)
                    after(act, wo_mm[c], j)
                    nc.scalar.copy(oT[c][:].rearrange("p k t -> p (k t)"), src[:]).then_inc(oT_done[c], 1)

                def step(i, own, cross, route, ahead):
                    if own:
                        exps("s", i)
                    if route:
                        act.wait_ge(g["lmax_done"], i - 1)
                        after(act, g["route_link"], ROUTE_LINKS * (i - 3) + 2)
                        nc.scalar.activation(gate_e[:], T[1][:, 0:EXPERTS], ACT.Exp, bias=lmax[:]
                                             ).then_inc(g["ex_done"], 1)
                    if own:
                        pT_half("s", i)
                        oT_copy("s", i, B)
                    if cross:
                        exps("x", i - 1)
                        pT_half("x", i - 1)
                    if ahead:
                        act.wait_ge(g["qT_tr"], i + 2)
                        after(act, scores_mm["s"], i + 1)
                        nc.scalar.mul(qT["s"][:].rearrange("p k t -> p (k t)"), A[:], INV_SQRT_HD
                                      ).then_inc(qT_done["s"], 1)
                    if cross:
                        oT_copy("x", i - 1, T[1])

                run_steps(act, step)

            @block.vector
            def _(dve):
                def flat(t):
                    return t[:].rearrange("p k t -> p (k t)")

                def norm_stats(c, j, src):
                    nc.vector.bn_stats(stats[c][:], src[:]).then_inc(stats_done[c], 1)
                    dve.wait_ge(stats_done[c], j + 1)
                    apart(dve)
                    nc.vector.bn_aggr(mv[c][:], stats[c][:]).then_inc(mv_done[c], 1)

                def normalise(c, j, src):
                    dve.wait_ge(rstd_done[c], j + 1)
                    nc.vector.tensor_scalar(xn[c][:], src[:], mv[c][:, 0:1], rstd[c][:], ALU.subtract,
                                            ALU.mult).then_inc(xn_done[c], 1)

                def row_max(c, j):
                    dve.wait_ge(scores_mm[c], j + 1)
                    after(dve, exp_done[c], HEADS * j)
                    nc.vector.tensor_reduce(nmax[c][:], S[:].rearrange("p r (k t) -> p (r k) t", k=KC), AX_X,
                                            ALU.max, negate=True).then_inc(nmax_done[c], 1)

                def invert_sums(c, j):
                    dve.wait_ge(exp_done[c], HEADS * (j + 1))
                    nc.vector.reciprocal(rinv[c][:], rsum[c][:]).then_inc(rinv_done[c], 1)

                def pT_half(c, j):
                    after(dve, pv_mm[c], j)
                    for r in (1, 3):
                        dve.wait_ge(pT_tr[c], 4 * j + r + 1)
                        nc.vector.tensor_copy(pT[c][:, 4 * r:4 * r + 4].rearrange("p h t -> p (h t)"), T[1][:]
                                              ).then_inc(pT_dve[c], 1)

                def scale_out(c, j, src):
                    dve.wait_ge(pv_mm[c], j + 1)
                    dve.wait_ge(rinv_done[c], j + 1)
                    after(dve, oT_tr[c], j)
                    nc.vector.tensor_tensor(
                        o[c][:].rearrange("p (k r d) -> p k r d", k=KC, r=4),
                        src[:].rearrange("p (k r d) -> p k r d", k=KC, r=4),
                        rinv[c][:].rearrange("p (r k) -> p k r", r=4).unsqueeze(3).to_broadcast([P, KC, 4, HD]),
                        ALU.mult).then_inc(o_done[c], 1)

                def link(j, n, ins):
                    ins.then_inc(g["route_link"], 1)
                    dve.wait_ge(g["route_link"], ROUTE_LINKS * j + n)

                nc.vector.memset(zeros_sb[:], 0.0).then_inc(g["zeroed"], 1)
                nc.vector.memset(chosen_cum[:], 0.0).then_inc(g["cum_zero"], 1)
                dve.wait_ge(g["consts_in"], 16 * 10)

                def step(i, own, cross, route, ahead):
                    if own:
                        row_max("s", i)
                    if route:
                        dve.wait_ge(xnT_tr["h"], i - 1)
                        after(dve, g["logits_mm"], i - 2)
                        nc.vector.tensor_copy(flat(xnT["h"]), T[0][:]).then_inc(xnT_done["h"], 1)
                    if cross:
                        dve.wait_ge(g["kx_mm"], i)
                        after(dve, scores_mm["x"], i - 1)
                        nc.vector.tensor_copy(flat(kT["x"]), A[:]).then_inc(kT_done["x"], 1)
                        dve.wait_ge(g["vx_mm"], i)
                        after(dve, pv_mm["x"], i - 1)
                        nc.vector.tensor_copy(v["x"][:], B[:]).then_inc(v_done["x"], 1)
                    if route:
                        dve.wait_ge(g["logits_mm"], i - 1)
                        after(dve, g["ex_done"], i - 2)
                        nc.vector.tensor_reduce(lmax[:], T[1][:, 0:EXPERTS], AX_X, ALU.max, negate=True
                                                ).then_inc(g["lmax_done"], 1)
                    if cross:
                        dve.wait_ge(xnT_tr["x"], i)
                        after(dve, g["qx_mm"], i - 1)
                        nc.vector.tensor_copy(flat(xnT["x"]), T[0][:]).then_inc(xnT_done["x"], 1)
                        dve.wait_ge(g["qx_mm"], i)
                        nc.vector.tensor_scalar(flat(qT["x"]), A[:], INV_SQRT_HD, None, ALU.mult
                                                ).then_inc(qT_done["x"], 1)
                    if own:
                        pT_half("s", i)
                        invert_sums("s", i)
                        scale_out("s", i, A)
                    if route:
                        j = i - 2
                        dve.wait_ge(g["ex_done"], i - 1)
                        after(dve, g["list_out"], 16 * TOP_K * (i - 2))
                        apart(dve)
                        link(j, 1, nc.vector.max(top_v[:], gate_e[:]))
                        apart(dve)
                        link(j, 2, nc.vector.max_index(top_i[:], top_v[:], gate_e[:]))
                        link(j, 3, nc.vector.tensor_reduce(top_s[:], top_v[:], AX_X, ALU.add))
                        link(j, 4, nc.vector.reciprocal(top_r[:], top_s[:]))
                        link(j, 5, nc.vector.tensor_scalar(rec[:].bitcast(F32)[:, :, 1], top_v[:], top_r[:],
                                                           1.0 / W_SCALE, ALU.mult, ALU.mult))
                        link(j, 6, nc.vector.tensor_copy(top_f[:], top_i[:]))
                        link(j, 7, nc.vector.tensor_tensor(
                            onehot[:], iota_e_sb[:].unsqueeze(1).to_broadcast([P, TOP_K, EXPERTS]),
                            top_f[:].unsqueeze(2).to_broadcast([P, TOP_K, EXPERTS]), ALU.is_equal))
                        with nc.allow_low_precision(reason="sums of zeros and ones are exact"):
                            link(j, 8, nc.vector.tensor_reduce(chosen[:], onehot[:].rearrange("p k e -> p e k"),
                                                               AX_X, ALU.add))
                    if own:
                        dve.wait_ge(wo_mm["s"], i + 1)
                        dve.wait_ge(g["resid_done"], i + 1)
                        after(dve, g["held_done"], i)
                        nc.vector.tensor_tensor(x1[:], A[:], resid[:], ALU.add).then_inc(g["x1_done"], 1)
                        dve.wait_ge(g["x1_done"], i + 1)
                        norm_stats("x", i, x1)
                    if ahead:
                        dve.wait_ge(g["x_in_s"], 16 * (i + 2))
                        norm_stats("s", i + 1, x_in)
                    if own:
                        after(dve, xnT_tr["x"], i)
                        normalise("x", i, x1)
                    if ahead:
                        after(dve, xnT_tr["s"], i + 1)
                        normalise("s", i + 1, x_in)
                    if route:
                        dve.wait_ge(g["rank_mm"], i - 1)
                        link(j, 9, nc.vector.tensor_tensor(chosen_cum[:], chosen_cum[:], chosen[:], ALU.add))
                        link(j, 10, nc.vector.tensor_tensor(row_of[:], B[:, 0:EXPERTS], rows0_sb[:], ALU.add))
                        link(j, 11, nc.vector.tensor_tensor(
                            row_sel[:], onehot[:], row_of[:].unsqueeze(1).to_broadcast([P, TOP_K, EXPERTS]),
                            ALU.mult))
                        link(j, 12, nc.vector.tensor_reduce(pos_f[:], row_sel[:], AX_X, ALU.add))
                        link(j, 13, nc.vector.tensor_copy(pos_u[:], pos_f[:]))
                        link(j, 14, nc.vector.tensor_copy(top_s[:], top_r[:]))
                    if cross:
                        row_max("x", i - 1)
                    if ahead:
                        dve.wait_ge(xnT_tr["s"], i + 2)
                        after(dve, g["v_mm"], i + 1)
                        nc.vector.tensor_copy(flat(xnT["s"]), T[0][:]).then_inc(xnT_done["s"], 1)
                        after(dve, g["rope_s_done"], 2 * (i + 1))
                        dve.wait_ge(g["q_mm"], i + 2)
                        nc.vector.tensor_tensor(qk[:, 0], A[:], bias_sb[:, 0], ALU.add).then_inc(g["qk_done"], 1)
                        dve.wait_ge(g["k_mm"], i + 2)
                        nc.vector.tensor_tensor(qk[:, 1], B[:], bias_sb[:, 1], ALU.add).then_inc(g["qk_done"], 1)
                        dve.wait_ge(g["qk_done"], 2 * (i + 2))
                        nc.vector.tensor_tensor(
                            rope_c[:].rearrange("p a (h d) -> p (a h) d", d=HD),
                            qk[:].rearrange("p a (h d) -> p (a h) d", d=HD),
                            rope_sb[:, 0].unsqueeze(1).to_broadcast([P, 2 * HEADS, HD]), ALU.mult
                        ).then_inc(g["rope_c_done"], 1)
                        dve.wait_ge(g["v_mm"], i + 2)
                        after(dve, pv_mm["s"], i + 1)
                        nc.vector.tensor_tensor(v["s"][:], T[1][:], bias_sb[:, 2], ALU.add).then_inc(v_done["s"], 1)
                        dve.wait_ge(g["rope_c_done"], i + 2)
                        dve.wait_ge(g["rope_s_done"], 2 * (i + 2))
                        after(dve, g["kT_tr"], i + 1)
                        nc.vector.tensor_tensor(qk_r[:], rope_c[:], rope_s[:], ALU.add).then_inc(g["rope_done"], 1)
                    if cross:
                        pT_half("x", i - 1)
                        invert_sums("x", i - 1)
                        scale_out("x", i - 1, T[0])
                    if ahead:
                        dve.wait_ge(g["kT_tr"], i + 2)
                        after(dve, scores_mm["s"], i + 1)
                        nc.vector.tensor_copy(flat(kT["s"]), B[:]).then_inc(kT_done["s"], 1)
                    if cross:
                        dve.wait_ge(wo_mm["x"], i)
                        dve.wait_ge(g["held_done"], i)
                        after(dve, g["x2_out"], 16 * (i - 1))
                        nc.vector.tensor_tensor(x2[:], T[0][:], x1_held[:], ALU.add).then_inc(g["x2_done"], 1)
                        dve.wait_ge(g["x2_done"], i)
                        norm_stats("h", i - 1, x2)
                        after(dve, xnT_tr["h"], i - 1)
                        after(dve, g["h_out"], 16 * (i - 1))
                        normalise("h", i - 1, x2)

                run_steps(dve, step)

            @block.gpsimd
            def _(pool):
                nc.gpsimd.memset(half_sb[:], -0.5).then_inc(g["half_set"], 1)
                pool.wait_ge(g["half_set"], 1)
                pool.wait_ge(g["consts_in"], 16 * 10)
                nc.gpsimd.tensor_copy(tok_f[:], iota_p_sb[:]).then_inc(g["tok_adv"], 1)
                pool.wait_ge(g["dump_out"], 16 * 3)

                def inv_std(c, j):
                    pool.wait_ge(mv_done[c], j + 1)
                    apart(pool)
                    nc.gpsimd.tensor_scalar(vare[c][:], mv[c][:, 1:2], EPS, None, ALU.add).then_inc(vare_done[c], 1)
                    pool.wait_ge(vare_done[c], j + 1)
                    nc.gpsimd.tensor_tensor(rstd[c][:], vare[c][:], half_sb[:], ALU.pow).then_inc(rstd_done[c], 1)

                def step(i, own, cross, route, ahead):
                    if own:
                        inv_std("x", i)
                    if ahead:
                        inv_std("s", i + 1)
                        pool.wait_ge(g["x_in_s"], 16 * (i + 2))
                        after(pool, g["x1_done"], i + 1)
                        nc.gpsimd.tensor_tensor(resid[:], x_in[:], bias_sb[:, 3], ALU.add
                                                ).then_inc(g["resid_done"], 1)
                        after(pool, g["rope_done"], i + 1)
                        pool.wait_ge(g["qk_done"], 2 * (i + 2))
                        src = qk[:].rearrange("p a (h s d) -> p (a h) s d", s=2, d=HD // 2)
                        dst = rope_s[:].rearrange("p a (h s d) -> p (a h) s d", s=2, d=HD // 2)
                        sin = rope_sb[:, 1].rearrange("p (s d) -> p s d", s=2)
                        for s in range(2):
                            nc.gpsimd.tensor_tensor(
                                dst[:, :, s], src[:, :, 1 - s],
                                sin[:, s].unsqueeze(1).to_broadcast([P, 2 * HEADS, HD // 2]), ALU.mult
                            ).then_inc(g["rope_s_done"], 1)
                    if route:
                        j = i - 2
                        after(pool, g["list_out"], 16 * TOP_K * (i - 2))
                        pool.wait_ge(g["tok_adv"], i - 1)
                        apart(pool)
                        nc.gpsimd.tensor_copy(rec[:, :, 0], tok_f[:].to_broadcast([P, TOP_K])
                                              ).then_inc(g["rec_tok"], 1)
                        pool.wait_ge(g["rec_tok"], i - 1)
                        apart(pool)
                        nc.gpsimd.tensor_scalar(tok_f[:], tok_f[:], float(TOK), None, ALU.add
                                                ).then_inc(g["tok_adv"], 1)
                        pool.wait_ge(g["route_link"], ROUTE_LINKS * j + 13)
                        apart(pool)
                        for k in range(TOP_K):
                            pool.indirect_dma_start(
                                out=list_dram[:, :], out_offset=bass.IndirectOffsetOnAxis(ap=pos_u[:, k:k + 1], axis=0),
                                in_=rec[:, k, :], in_offset=None).then_inc(g["list_out"], 16)
                    if cross:
                        inv_std("h", i - 1)
                    if own:
                        pool.wait_ge(g["x1_done"], i + 1)
                        after(pool, g["x2_done"], i)
                        apart(pool)
                        nc.gpsimd.tensor_copy(x1_held[:], x1[:]).then_inc(g["held_done"], 1)

                run_steps(pool, step)

        cnt = sb("cnt", [P, EXPERTS])
        cnt_i = sb("cnt_i", [P, EXPERTS], I32)
        cnt_s = sb("cnt_s", [P, EXPERTS], I32)
        ntile = sb("ntile", [P, EXPERTS])
        ncum = sb("ncum", [P, EXPERTS])
        passed = sb("passed", [P, EXPERTS])
        passed_n = sb("passed_n", [P, EXPERTS])
        tab_e = sb("tab_e", [P, 1])
        tab_a = sb("tab_a", [P, 1])
        tab_b = sb("tab_b", [P, 1])
        tab_c = sb("tab_c", [P, 1])
        tab = sb("tab", [P, 2], I32)
        tab_row = sb("tab_row", [1, 2 * P], I32)
        wa_in = [sb(f"wa_in{s}", [P, WA]) for s in range(2)]
        wb_in = [sb(f"wb_in{s}", [MB, D]) for s in range(2)]
        wa = {(n, s): sb(f"wa_{n}{s}", [P, WA], F16) for n in ("hi", "lo") for s in range(ROW_AHEAD)}
        wb = {(n, s): sb(f"wb_{n}{s}", [MB, D], F16) for n in ("hi", "lo") for s in range(ROW_AHEAD)}
        lst = [sb(f"lst{s}", [P, SUBS, 2], U32) for s in range(RING)]
        xg = [sb(f"xg{s}", [P, SUBS, D]) for s in range(ROW_AHEAD)]
        xgT = {(n, s): sb(f"xgT_{n}{s}", [P, KC, TILE], F16) for n in ("hi", "lo") for s in range(2)}
        silu_a = sb("silu_a", [P, TILE])
        silu_b = sb("silu_b", [MB, TILE])
        mid_a = sb("mid_a", [P, TILE])
        mid_b = sb("mid_b", [MB, TILE])
        ma = {n: sb(f"ma_{n}", [P, TILE], F16) for n in ("hi", "lo")}
        mb = {n: sb(f"mb_{n}", [MB, TILE], F16) for n in ("hi", "lo")}
        y = [sb(f"y{s}", [P, SUBS, D]) for s in range(2)]
        GU = ((S[:, 2], S[:, 3]), (A, B))
        PARTS = (("hi", "hi"), ("hi", "lo"), ("lo", "hi"))

        block2 = ctx.enter_context(nc.Block())
        GROUPS = MOE_TILES // RING

        def run_tiles(eng, tile):
            for u in range(RING):
                tile(u, u, 0, RING)
            with eng.Fori(1, GROUPS - 1) as n:
                for u in range(RING):
                    tile(n * RING + u, u, n, RING)
            for u in range(RING):
                tile((GROUPS - 1) * RING + u, u, GROUPS - 1, RING - 1 - u)

        @block2.sync
        def _(sp):
            sp.wait_ge(m["tab_link"], 13)
            sp.dma_start(tab_dram, tab[:]).then_inc(m["tab_out"], 16)
            sp.wait_ge(m["tab_out"], 16)
            sp.dma_start(tab_row[:], tab_dram.rearrange("(o p) c -> o (p c)", o=1)).then_inc(m["tab_in"], 16)
            sp.wait_ge(m["tab_in"], 16)
            sp.wait_ge(g["list_out"], 16 * TOP_K * SEQS)

            def load_list(t, u):
                r = sp.value_load(tab_row[0:1, bass.ds(2 * t + 1, 1)], min_val=0, max_val=LIST_ROWS - TILE)
                after(sp, m["added"], 16 * SUBS * (t - RING + 1))
                sp.dma_start(lst[u][:], list_dram[bass.ds(r, TILE), :].rearrange("(s p) c -> p s c", s=SUBS)
                             ).then_inc(m[f"l{u}_in"], 16)

            def load_weights(t, u):
                e = sp.value_load(tab_row[0:1, bass.ds(2 * t, 1)], min_val=0, max_val=EXPERTS - 1)
                after(sp, m["wa_lo_done"], t - 1)
                after(sp, m["wb_lo_done"], t - 1)
                sp.dma_start(wa_in[u % 2][:], w_a[bass.ds(e, 1)].rearrange("a p n -> (a p) n")
                             ).then_inc(m[f"w{u % 2}_in"], 16)
                sp.dma_start(wb_in[u % 2][:], w_b[bass.ds(e, 1)].rearrange("a p n -> (a p) n")
                             ).then_inc(m[f"w{u % 2}_in"], 16)

            load_list(0, 0)
            load_weights(0, 0)
            load_list(1, 1)
            load_weights(1, 1)
            for u in range(2, LIST_AHEAD):
                load_list(u, u)
            for u in range(2, SPLIT_AHEAD + 1):
                load_weights(u, u)

            def tile(t, u, n, left):
                if left >= LIST_AHEAD:
                    load_list(t + LIST_AHEAD, (u + LIST_AHEAD) % RING)
                if left >= SPLIT_AHEAD + 1:
                    load_weights(t + SPLIT_AHEAD + 1, u + SPLIT_AHEAD + 1)

            run_tiles(sp, tile)
            sp.wait_ge(m["added"], 16 * SUBS * MOE_TILES)
            sp.wait_ge(g["x2_out"], 16 * SEQS)
            sp.wait_ge(g["h_out"], 16 * SEQS)

        @block2.gpsimd
        def _(pool):
            pool.wait_ge(g["h_out"], 16 * SEQS)
            pool.wait_ge(g["x2_out"], 16 * SEQS)

            def gather(t, u, n):
                after(pool, m["xT_mm"], 2 * (t - ROW_AHEAD + 1))
                pool.wait_ge(m[f"l{u}_in"], 16 * (n + 1))
                apart(pool)
                for q in range(SUBS):
                    pool.indirect_dma_start(
                        out=xg[u % ROW_AHEAD][:, q], out_offset=None, in_=h_dram[:, :],
                        in_offset=bass.IndirectOffsetOnAxis(ap=lst[u][:, q, 0:1], axis=0)
                    ).then_inc(m[f"g{u % ROW_AHEAD}_in"], 16)

            def weights_hi(t, u, n):
                pool.wait_ge(m[f"w{u % 2}_in"], 32 * (RING // 2 * n + u // 2 + 1))
                after(pool, m["dn_mm"], SUBS * (t - ROW_AHEAD + 1))
                apart(pool)
                nc.gpsimd.tensor_scalar(wb["hi", u % ROW_AHEAD][:], wb_in[u % 2][:], W_SCALE, None, ALU.mult
                                        ).then_inc(m["wb_hi_done"], 1)

            gather(0, 0, 0)
            gather(1, 1, 0)
            for u in range(SPLIT_AHEAD):
                weights_hi(u, u, 0)
            for u in range(2, ROW_AHEAD):
                gather(u, u, 0)

            def tile(t, u, n, left):
                if left >= SPLIT_AHEAD:
                    weights_hi(t + SPLIT_AHEAD, (u + SPLIT_AHEAD) % RING, n + (u + SPLIT_AHEAD) // RING)
                if left >= ROW_AHEAD:
                    gather(t + ROW_AHEAD, (u + ROW_AHEAD) % RING, n + (u + ROW_AHEAD) // RING)
                after(pool, m["added"], 16 * SUBS * t)
                pool.wait_ge(m["y_act"], t + 1)
                pool.wait_ge(m["y_dve"], t + 1)
                apart(pool)
                for q in range(SUBS):
                    pool.indirect_dma_start(
                        out=out[:, :], out_offset=bass.IndirectOffsetOnAxis(ap=lst[u][:, q, 0:1], axis=0),
                        in_=y[u % 2][:, q], in_offset=None, compute_op=ALU.add).then_inc(m["added"], 16)

            run_tiles(pool, tile)

        @block2.tensor
        def _(pe):
            pe.wait_ge(g["route_link"], ROUTE_LINKS * SEQS)
            nc.tensor.matmul(A[:, 0:EXPERTS], onesb_sb[:], chosen_cum[:], start=True, stop=True
                             ).then_inc(m["cum_mm"], 1)

            def turn(t, u, n):
                pe.wait_ge(m[f"g{u % ROW_AHEAD}_in"], 16 * SUBS * (RING // ROW_AHEAD * n + u // ROW_AHEAD + 1))
                for h in range(2):
                    after(pe, m["xT_lo_done"], 2 * (t - 1) + h + 1)
                    for k in (2 * h, 2 * h + 1):
                        for q in range(SUBS):
                            mm = nc.tensor.transpose(S[:, h, (k % 2) * TILE + q * P:(k % 2) * TILE + (q + 1) * P],
                                                     xg[u % ROW_AHEAD][:, q, k * P:(k + 1) * P], ident_sb[:])
                    mm.then_inc(m["xT_mm"], 1)

            def gate_up(t, u):
                first, second = GU[u % 2]
                pe.wait_ge(m["xT_lo_done"], 2 * (t + 1))
                pe.wait_ge(m["wa_lo_done"], t + 1)
                after(pe, m["mid_done"], 2 * (t - 1))
                for c, dst in ((0, first[:, 0:TILE]), (1, first[:, TILE:2 * TILE]), (2, second[:, 0:TILE])):
                    for k in range(KC):
                        for i, (wn, xn_) in enumerate(PARTS):
                            w = wa[wn, u % ROW_AHEAD][:, k * 2 * MID + c * P:k * 2 * MID + (c + 1) * P]
                            mm = nc.tensor.matmul(dst, w, xgT[xn_, u % 2][:, k], start=(k == 0 and i == 0),
                                                  stop=(k == KC - 1 and i == len(PARTS) - 1))
                    if c:
                        mm.then_inc(m["gu_mm"], 1)

            def down(t, u):
                pe.wait_ge(m["wb_lo_done"], t + 1)
                for q in range(SUBS):
                    after(pe, m["y_dve" if q else "y_act"], t)
                    cols = slice(q * P, (q + 1) * P)
                    pe.wait_ge(m["mid_lo_done"], 2 * t + 1)
                    for i, (mn, wn) in enumerate(PARTS):
                        nc.tensor.matmul(T[q][:], ma[mn][:, cols], wa[wn, u % ROW_AHEAD][:, 2 * MID * KC:],
                                         start=(i == 0), stop=False)
                    pe.wait_ge(m["mid_lo_done"], 2 * t + 2)
                    for i, (mn, wn) in enumerate(PARTS):
                        mm = nc.tensor.matmul(T[q][:], mb[mn][:, cols], wb[wn, u % ROW_AHEAD][:], start=False,
                                              stop=(i == len(PARTS) - 1))
                    mm.then_inc(m["dn_mm"], 1)

            turn(0, 0, 0)
            gate_up(0, 0)
            turn(1, 1, 0)

            def tile(t, u, n, left):
                if left >= 2:
                    turn(t + 2, (u + 2) % RING, n + (u + 2) // RING)
                if left >= 1:
                    gate_up(t + 1, u + 1)
                down(t, u)

            run_tiles(pe, tile)

        @block2.scalar
        def _(act):
            def weights_hi(t, u, n):
                act.wait_ge(m[f"w{u % 2}_in"], 32 * (RING // 2 * n + u // 2 + 1))
                after(act, m["dn_mm"], SUBS * (t - ROW_AHEAD + 1))
                nc.scalar.mul(wa["hi", u % ROW_AHEAD][:], wa_in[u % 2][:], W_SCALE).then_inc(m["wa_hi_done"], 1)

            def xT_hi(t, s):
                for h in range(2):
                    act.wait_ge(m["xT_mm"], 2 * t + h + 1)
                    after(act, m["gu_mm"], 2 * (t - 1))
                    nc.scalar.copy(xgT["hi", s][:, 2 * h:2 * h + 2].rearrange("p k t -> p (k t)"), S[:, h]
                                   ).then_inc(m["xT_hi_done"], 1)

            def weigh(t, u):
                act.wait_ge(m["dn_mm"], 2 * t + 1)
                after(act, m["added"], 16 * SUBS * (t - 1))
                nc.scalar.activation(y[u % 2][:, 0], T[0][:], ACT.Copy, scale=lst[u % RING][:].bitcast(F32)[:, 0, 1:2]
                                     ).then_inc(m["y_act"], 1)

            weights_hi(0, 0, 0)
            xT_hi(0, 0)
            weights_hi(1, 1, 0)
            xT_hi(1, 1)
            weights_hi(2, 2, 0)

            def tile(t, u, n, left):
                first, second = GU[u % 2]
                for c, dst, src in ((1, silu_a, first[:, 0:TILE]), (2, silu_b, second[0:MB, 0:TILE])):
                    act.wait_ge(m["gu_mm"], 2 * t + c)
                    after(act, m["mid_done"], 2 * (t - 1) + c)
                    nc.scalar.activation(dst[:], src, ACT.Silu, scale=1.0 / W_SCALE).then_inc(m["silu_done"], 1)
                if not (isinstance(t, int) and t == 0):
                    weigh(t - 1, u - 1)
                if left >= 2:
                    xT_hi(t + 2, u % 2)
                for c, hi, src in ((1, ma["hi"], mid_a), (2, mb["hi"], mid_b)):
                    act.wait_ge(m["mid_done"], 2 * t + c)
                    after(act, m["dn_mm"], SUBS * t)
                    nc.scalar.copy(hi[:], src[:]).then_inc(m["mid_hi_done"], 1)
                if left >= SPLIT_AHEAD:
                    weights_hi(t + SPLIT_AHEAD, (u + SPLIT_AHEAD) % RING, n + (u + SPLIT_AHEAD) // RING)

            run_tiles(act, tile)
            weigh(MOE_TILES - 1, RING - 1)

        @block2.vector
        def _(dve):
            def link(n, ins):
                ins.then_inc(m["tab_link"], 1)
                dve.wait_ge(m["tab_link"], n)

            dve.wait_ge(m["cum_mm"], 1)
            link(1, nc.vector.tensor_scalar(cnt[:], A[:, 0:EXPERTS], float(TILE - 1), None, ALU.add))
            link(2, nc.vector.tensor_copy(cnt_i[:], cnt[:]))
            link(3, nc.vector.tensor_scalar(cnt_s[:], cnt_i[:], TILE.bit_length() - 1, None,
                                            ALU.arith_shift_right))
            link(4, nc.vector.tensor_copy(ntile[:], cnt_s[:]))
            link(5, nc.vector.tensor_tensor_scan(ncum[:], zeros_sb[:, 0:EXPERTS], ntile[:], 0.0, ALU.add, ALU.add))
            link(6, nc.vector.tensor_scalar(passed[:], ncum[:], iota_p_sb[:], None, ALU.is_le))
            link(7, nc.vector.tensor_tensor(passed_n[:], passed[:], ntile[:], ALU.mult))
            link(8, nc.vector.tensor_reduce(tab_e[:], passed[:], AX_X, ALU.add))
            link(9, nc.vector.tensor_reduce(tab_a[:], passed_n[:], AX_X, ALU.add))
            link(10, nc.vector.tensor_scalar(tab_b[:], tab_a[:], iota_p_sb[:], -float(TILE), ALU.subtract, ALU.mult))
            link(11, nc.vector.scalar_tensor_tensor(tab_c[:], tab_e[:], float(TOKENS), tab_b[:], ALU.mult, ALU.add))
            link(12, nc.vector.tensor_scalar(tab[:, 1:2], tab_c[:], float(EXPERTS * TOKENS), None, ALU.min))
            link(13, nc.vector.tensor_scalar(tab[:, 0:1], tab_e[:], float(EXPERTS - 1), None, ALU.min))

            def weights_lo(t, u):
                w = u % ROW_AHEAD
                after(dve, m["dn_mm"], SUBS * (t - ROW_AHEAD + 1))
                dve.wait_ge(m["wa_hi_done"], t + 1)
                nc.vector.scalar_tensor_tensor(wa["lo", w][:], wa_in[u % 2][:], W_SCALE, wa["hi", w][:], ALU.mult,
                                               ALU.subtract).then_inc(m["wa_lo_done"], 1)

            def last_rows_lo(t, u):
                w = u % ROW_AHEAD
                dve.wait_ge(m["wb_hi_done"], t + 1)
                nc.vector.scalar_tensor_tensor(wb["lo", w][:], wb_in[u % 2][:], W_SCALE, wb["hi", w][:], ALU.mult,
                                               ALU.subtract).then_inc(m["wb_lo_done"], 1)

            def xT_lo(t, s):
                for h in range(2):
                    dve.wait_ge(m["xT_hi_done"], 2 * t + h + 1)
                    after(dve, m["gu_mm"], 2 * (t - 1))
                    cols = slice(2 * h, 2 * h + 2)
                    nc.vector.tensor_tensor(xgT["lo", s][:, cols].rearrange("p k t -> p (k t)"), S[:, h],
                                            xgT["hi", s][:, cols].rearrange("p k t -> p (k t)"), ALU.subtract
                                            ).then_inc(m["xT_lo_done"], 1)

            def weigh(t, u):
                dve.wait_ge(m["dn_mm"], 2 * t + 2)
                after(dve, m["added"], 16 * SUBS * (t - 1))
                nc.vector.tensor_scalar(y[u % 2][:, 1], T[1][:], lst[u % RING][:].bitcast(F32)[:, 1, 1:2], None,
                                        ALU.mult).then_inc(m["y_dve"], 1)

            weights_lo(0, 0)
            xT_lo(0, 0)
            last_rows_lo(0, 0)
            weights_lo(1, 1)
            xT_lo(1, 1)
            last_rows_lo(1, 1)
            weights_lo(2, 2)

            def tile(t, u, n, left):
                first, second = GU[u % 2]
                for c, dst, src, gate in ((1, mid_a, first[:, TILE:2 * TILE], silu_a),
                                          (2, mid_b, second[MB:2 * MB, 0:TILE], silu_b)):
                    dve.wait_ge(m["silu_done"], 2 * t + c)
                    after(dve, m["mid_lo_done"], 2 * (t - 1) + c)
                    nc.vector.scalar_tensor_tensor(dst[:], src, 1.0 / W_SCALE, gate[:], ALU.mult, ALU.mult
                                                   ).then_inc(m["mid_done"], 1)
                if not (isinstance(t, int) and t == 0):
                    weigh(t - 1, u - 1)
                if left >= 2:
                    xT_lo(t + 2, u % 2)
                for c, lo, hi, src in ((1, ma["lo"], ma["hi"], mid_a), (2, mb["lo"], mb["hi"], mid_b)):
                    dve.wait_ge(m["mid_hi_done"], 2 * t + c)
                    after(dve, m["dn_mm"], SUBS * t)
                    nc.vector.tensor_tensor(lo[:], src[:], hi[:], ALU.subtract).then_inc(m["mid_lo_done"], 1)
                if left >= SPLIT_AHEAD - 1:
                    last_rows_lo(t + SPLIT_AHEAD - 1, u + SPLIT_AHEAD - 1)
                if left >= SPLIT_AHEAD:
                    weights_lo(t + SPLIT_AHEAD, u + SPLIT_AHEAD)

            run_tiles(dve, tile)
            weigh(MOE_TILES - 1, RING - 1)


def kernel(**inputs):
    import ml_dtypes
    import numpy as np
    import concourse.bacc as bacc
    from concourse.bass_utils import run_bass_kernel_spmd

    a = {k: np.ascontiguousarray(np.asarray(v)) for k, v in inputs.items()}

    def by_rows(w):
        return w.reshape(w.shape[0] // P, P, w.shape[1]).transpose(1, 0, 2)

    w_attn = np.stack([by_rows(a[n].T) for n in ("L0_attn_Wq", "L0_attn_Wk", "L0_attn_Wv", "L0_attn_Wo",
                                                 "L0_xattn_Wq", "L0_xattn_Wout")], axis=1)
    gate, up = a["L0_ffn_gate_proj"], a["L0_ffn_up_proj"]
    gu = np.concatenate([gate[:, :, :P], up[:, :, :P], gate[:, :, P:], up[:, :, P:]], axis=2)
    gu = gu.reshape(EXPERTS, KC, P, 2 * MID).transpose(0, 2, 1, 3).reshape(EXPERTS, P, -1)
    down = a["L0_ffn_down_proj"]
    w_a = np.concatenate([gu, down[:, :P]], axis=2)
    biases = np.broadcast_to(np.stack([a[n] for n in ("L0_attn_bq", "L0_attn_bk", "L0_attn_bv", "L0_attn_bo")]),
                             (P, 4, D))
    half = HD // 2
    freq = (1.0 / 10000.0 ** (np.arange(half, dtype=np.float32) / np.float32(half))).astype(np.float32)
    ang = np.arange(TOK, dtype=np.float32)[:, None] * freq[None, :]
    cos, sin = np.cos(ang), np.sin(ang)
    rope = np.stack([np.concatenate([cos, cos], 1), np.concatenate([-sin, sin], 1)], axis=1)
    t = np.arange(P)
    causal = np.tile(np.where(t[None, :] > t[:, None], -1e30, 0.0), (1, 4))
    fill = np.zeros((LIST_ROWS, 2), np.uint32)
    fill[:, 0] = TOKENS + np.arange(LIST_ROWS) % DUMP
    arrays = {
        "x": a["x"], "ctxT": a["ctx_512"].transpose(0, 2, 1), "w_attn": w_attn,
        "w_kv": a["L0_xattn_Wkv_expand"].T, "w_gate": by_rows(a["L0_ffn_gate_kernel"]),
        "w_a": w_a, "w_b": down[:, P:], "biases": biases,
        "ident": np.eye(P, dtype=np.float32), "identb": np.eye(P).astype(ml_dtypes.bfloat16),
        "rope": rope.astype(np.float32), "causal": causal.astype(ml_dtypes.bfloat16),
        "upper": (t[:, None] < t[None, :]).astype(ml_dtypes.bfloat16),
        "onesb": np.ones((P, P), ml_dtypes.bfloat16),
        "iota_e": np.broadcast_to(np.arange(EXPERTS, dtype=np.float32), (P, EXPERTS)),
        "list_rows0": np.broadcast_to(np.arange(EXPERTS, dtype=np.float32) * TOKENS, (P, EXPERTS)),
        "iota_p": t[:, None].astype(np.float32), "list_fill": fill.reshape(P, -1),
    }
    arrays = {k: np.ascontiguousarray(v) for k, v in arrays.items()}
    nc = bacc.Bacc("TRN2", target_bir_lowering=False, num_devices=1)
    args = [nc.dram_tensor(k, v.shape, mybir.dt.from_np(v.dtype), kind="ExternalInput").ap()
            for k, v in arrays.items()]
    out = nc.dram_tensor("out_rows", (TOKENS + DUMP, D), F32, kind="ExternalOutput").ap()
    build(nc, *args, out)
    r = run_bass_kernel_spmd(nc, [arrays], core_ids=[0])
    return r.results[0]["out_rows"][:TOKENS].reshape(SEQS, TOK, D)
```

```python
from contextlib import ExitStack

import concourse.bass as bass
from concourse import mybir

ALU = mybir.AluOpType
ACT = mybir.ActivationFunctionType
AX_X = mybir.AxisListType.X
F32 = mybir.dt.float32
BF16 = mybir.dt.bfloat16
F16 = mybir.dt.float16
U32 = mybir.dt.uint32
I32 = mybir.dt.int32

P = 128
SEQS, TOK, D = 16, 128, 512
HEADS, HD = 16, 32
KC = D // P
EXPERTS, TOP_K, MID = 32, 8, 192
TOKENS = SEQS * TOK
TILE = 256
SUBS = TILE // P
LIST_ROWS = EXPERTS * TOKENS + TILE
RING = 8
MOE_TILES = (TOKENS * TOP_K + EXPERTS * (TILE - 1)) // TILE
LIST_AHEAD, ROW_AHEAD, LOAD_AHEAD, SPLIT_AHEAD = 6, 4, 6, 3
MB = MID - P
GU_COLS = KC * 2 * MID
W_COLS = GU_COLS + 2 * D
W_SCALE = 64.0
PARTS = (("hi", "hi"), ("hi", "lo"), ("lo", "hi"))
PRODUCTS = KC * len(PARTS)
DUMP = TILE
INV_SQRT_HD = float(HD) ** -0.5
EPS = 1e-5
ROUTE_LINKS = 13


def after(eng, sem, count):
    if isinstance(count, int) and count <= 0:
        return
    eng.wait_ge(sem, count)


def apart(eng):
    eng.nop(nofuse=True)


def build(nc, x, ctxT, w_attn, w_kv, w_gate, w_expert, biases, ident, identb, rope, causal,
          upper, onesb, iota_e, list_rows0, iota_p, list_fill, out):
    with ExitStack() as ctx:
        def sb(name, shape, dt=F32):
            return ctx.enter_context(nc.sbuf_tensor(name, shape, dt))

        def sem(name):
            return ctx.enter_context(nc.semaphore(name))

        h_dram = nc.dram_tensor("h_rows", (TOKENS + DUMP, D), F32, kind="Internal").ap()
        list_dram = nc.dram_tensor("expert_lists", (LIST_ROWS, 2), U32, kind="Internal").ap()
        tab_dram = nc.dram_tensor("tile_table", (P, 2), I32, kind="Internal").ap()

        S = ctx.enter_context(nc.psum_tensor("scores_ps", [P, 4, 512], F32))
        T = [ctx.enter_context(nc.psum_tensor(f"t{n}_ps", [P, 512], F32)) for n in range(2)]
        A = ctx.enter_context(nc.psum_tensor("a_ps", [P, 512], F32))
        B = ctx.enter_context(nc.psum_tensor("b_ps", [P, 512], F32))

        PT_BANK = {"s": (T[0], T[1], B, T[1]), "x": (A, B, T[0], T[1])}

        ident_sb = sb("ident_sb", [P, P])
        identb_sb = sb("identb_sb", [P, P], BF16)
        rope_sb = sb("rope_sb", [P, 2, HD])
        causal_sb = sb("causal_sb", [P, 512], BF16)
        upper_sb = sb("upper_sb", [P, P], BF16)
        onesb_sb = sb("onesb_sb", [P, P], BF16)
        iota_e_sb = sb("iota_e_sb", [P, EXPERTS])
        rows0_sb = sb("rows0_sb", [P, EXPERTS])
        iota_p_sb = sb("iota_p_sb", [P, 1])
        bias_sb = sb("bias_sb", [P, 4, D])
        zeros_sb = sb("zeros_sb", [P, 2 * D])
        chosen_cum = sb("chosen_cum", [P, EXPERTS], BF16)
        half_sb = sb("half_sb", [P, 1])
        cnt = sb("cnt", [P, EXPERTS])
        cnt_i = sb("cnt_i", [P, EXPERTS], I32)
        cnt_s = sb("cnt_s", [P, EXPERTS], I32)
        ntile = sb("ntile", [P, EXPERTS])
        ncum = sb("ncum", [P, EXPERTS])
        passed = sb("passed", [P, EXPERTS])
        passed_n = sb("passed_n", [P, EXPERTS])
        tab_e = sb("tab_e", [P, 1])
        tab_a = sb("tab_a", [P, 1])
        tab_b = sb("tab_b", [P, 1])
        tab_c = sb("tab_c", [P, 1])
        tab = sb("tab", [P, 2], I32)
        tab_row = sb("tab_row", [1, 2 * P], I32)
        we_in = [sb(f"we_in{s}", [P, W_COLS]) for s in range(2)]
        we = {(n, s): sb(f"we_{n}{s}", [P, W_COLS], F16) for n in ("hi", "lo") for s in range(2)}

        def sems(names):
            return {n: sem(n) for n in names.split()}
        g = sems("ident_in consts_in w0_stage w1_stage w_rest_in w_hi_done w_lo_done zeroed dump_out half_set "
                 "cum_zero x_in_s x_res_in resid_done ctx_in_s q_mm k_mm v_mm kx_mm vx_mm qx_mm q_done k_done "
                 "rope_s_done rope_c_done rope_done ctx_hi ctx_done qT_tr kT_tr x1_done held_done x2_done x2_out h_out logits_mm "
                 "lmax_done ex_done route_link rank_mm rec_tok tok_adv list_out")
        xn_done, xnT_tr, xnT_hi, xnT_done, stats_done, mv_done, vare_done, rstd_done = (
            {c: sem(f"{n}_{c}") for c in "sxh"} for n in
            ("xn_done", "xnT_tr", "xnT_hi", "xnT_done", "stats_done", "mv_done", "vare_done", "rstd_done"))
        qT_hi, kT_hi, qT_done, kT_done, v_done, scores_mm, nmax_done, exp_done, pT_tr, pT_act, pT_dve, rinv_done, pv_mm, \
            o_done, oT_tr, oT_hi, oT_done, wo_mm = (
                {c: sem(f"{n}_{c}") for c in "sx"} for n in
                ("qT_hi", "kT_hi", "qT_done", "kT_done", "v_done", "scores_mm", "nmax_done", "exp_done", "pT_tr", "pT_act",
                 "pT_dve", "rinv_done", "pv_mm", "o_done", "oT_tr", "oT_hi", "oT_done", "wo_mm"))
        m = sems("cum_mm tab_link tab_out tab_in w0_in w1_in w2_in w3_in l0_in l1_in l2_in l3_in l4_in l5_in l6_in l7_in g0_in g1_in g2_in g3_in "
                 "we_hi_done we_lo_done xT_mm xT_hi_done xT_lo_done gu_mm silu_done "
                 "mid_done mid_hi_done mid_lo_done dn_mm y_act y_dve added")

        FIRST, LAST = 4, SEQS - 1

        def run_steps(eng, step, between=lambda: None):
            def alone(i):
                step(i, i + 1 < SEQS, 0 <= i < SEQS, 0 <= i - 1 < SEQS, 0 <= i - 2 < SEQS, 0 <= i - 3 < SEQS)
            alone(-1)
            between()
            for i in range(FIRST):
                alone(i)
            with eng.Fori(FIRST, LAST) as i:
                step(i, True, True, True, True, True)
            for i in range(LAST, SEQS + 3):
                alone(i)

        def load_weights(sp, t, u):
            e = sp.value_load(tab_row[0:1, bass.ds(2 * t, 1)], min_val=0, max_val=EXPERTS - 1)
            after(sp, m["we_lo_done"], t - ROW_AHEAD + 1)
            sp.dma_start(we_in[u % ROW_AHEAD][:], w_expert[bass.ds(e, 1)].rearrange("a p n -> (a p) n")
                         ).then_inc(m[f"w{u % ROW_AHEAD}_in"], 16)

        def weights_hi(act, t, u, n):
            act.wait_ge(m[f"w{u % ROW_AHEAD}_in"], 16 * (RING // ROW_AHEAD * n + u // ROW_AHEAD + 1))
            after(act, m["dn_mm"], SUBS * (t - ROW_AHEAD + 1))
            nc.scalar.mul(we["hi", u % ROW_AHEAD][:], we_in[u % ROW_AHEAD][:], W_SCALE).then_inc(m["we_hi_done"], 1)

        def weights_lo(dve, t, u):
            after(dve, m["dn_mm"], SUBS * (t - ROW_AHEAD + 1))
            dve.wait_ge(m["we_hi_done"], t + 1)
            nc.vector.scalar_tensor_tensor(we["lo", u % ROW_AHEAD][:], we_in[u % ROW_AHEAD][:], W_SCALE,
                                           we["hi", u % ROW_AHEAD][:], ALU.mult, ALU.subtract
                                           ).then_inc(m["we_lo_done"], 1)

        with ExitStack() as wctx:
            def wsb(name, shape, dt=F32):
                return wctx.enter_context(nc.sbuf_tensor(name, shape, dt))
            w = {(n, p): wsb(f"w{n}_{p}", [P, KC, D], F16) for n in range(6) for p in ("hi", "lo")}
            w_kv_p = {p: wsb(f"w_kv_{p}", [P, 2 * D], F16) for p in ("hi", "lo")}
            w_gate_sb = wsb("w_gate_sb", [P, KC, EXPERTS])
            x_in = wsb("x_in", [P, D])
            resid = wsb("resid", [P, D])
            xn = {c: wsb(f"xn_{c}", [P, D]) for c in "sxh"}
            xnT = {(c, n): wsb(f"xnT_{c}{n}", [P, KC, P], F16) for c in "sx" for n in ("hi", "lo")}
            hT = wsb("hT", [P, KC, P])
            x_res = wsb("x_res", [P, D])
            stats = {c: wsb(f"stats_{c}", [P, 6]) for c in "sxh"}
            mv = {c: wsb(f"mv_{c}", [P, 2]) for c in "sxh"}
            vare = {c: wsb(f"vare_{c}", [P, 1]) for c in "sxh"}
            rstd = {c: wsb(f"rstd_{c}", [P, 1]) for c in "sxh"}
            qk = wsb("qk", [P, 2, D])
            rope_c = wsb("rope_c", [P, 2, D])
            rope_s = wsb("rope_s", [P, 2, D])
            qk_r = wsb("qk_r", [P, 2, D])
            ctx_in = wsb("ctx_in", [P, P])
            ctx_p = {p: wsb(f"ctx_{p}", [P, P], F16) for p in ("hi", "lo")}
            qT = {(c, n): wsb(f"qT_{c}{n}", [P, KC, P], F16) for c in "sx" for n in ("hi", "lo")}
            kT = {(c, n): wsb(f"kT_{c}{n}", [P, KC, P], F16) for c in "sx" for n in ("hi", "lo")}
            v = {c: wsb(f"v_{c}", [P, D]) for c in "sx"}
            nmax = {c: wsb(f"nmax_{c}", [P, HEADS]) for c in "sx"}
            rsum = {c: wsb(f"rsum_{c}", [P, HEADS]) for c in "sx"}
            rinv = {c: wsb(f"rinv_{c}", [P, HEADS]) for c in "sx"}
            probs = {c: wsb(f"probs_{c}", [P, HEADS, TOK]) for c in "sx"}
            pT = {c: wsb(f"pT_{c}", [P, HEADS, TOK]) for c in "sx"}
            o = {c: wsb(f"o_{c}", [P, D]) for c in "sx"}
            oT = {(c, n): wsb(f"oT_{c}{n}", [P, KC, P], F16) for c in "sx" for n in ("hi", "lo")}
            x1 = wsb("x1", [P, D])
            x1_held = wsb("x1_held", [P, D])
            x2 = wsb("x2", [P, D])
            lmax = wsb("lmax", [P, 1])
            gate_e = wsb("gate_e", [P, EXPERTS])
            top_v = wsb("top_v", [P, TOP_K])
            top_i = wsb("top_i", [P, TOP_K], U32)
            top_f = wsb("top_f", [P, TOP_K])
            top_s = wsb("top_s", [P, 1])
            top_r = wsb("top_r", [P, 1])
            onehot = wsb("onehot", [P, TOP_K, EXPERTS])
            chosen = wsb("chosen", [P, EXPERTS], BF16)
            row_of = wsb("row_of", [P, EXPERTS])
            row_sel = wsb("row_sel", [P, TOP_K, EXPERTS])
            pos_f = wsb("pos_f", [P, TOP_K])
            pos_u = wsb("pos_u", [P, TOP_K], U32)
            rec = wsb("rec", [P, TOP_K, 2], U32)
            tok_f = wsb("tok_f", [P, 1])

            block = wctx.enter_context(nc.Block())

            def flat(t):
                return t[:].rearrange("p k t -> p (k t)")

            @block.sync
            def _(sp):
                sp.dma_start(ident_sb[:], ident).then_inc(g["ident_in"], 16)

                def of(t, b):
                    return t[b] if isinstance(b, int) else t[bass.ds(b, 1)].rearrange("a t d -> (a t) d")

                def stage(n):
                    after(sp, g["w_lo_done"], n - 1)
                    sp.dma_start(we_in[n % 2][:, 0:KC * D], w_attn[:, n].rearrange("p k d -> p (k d)")).then_inc(g[f"w{n % 2}_stage"], 16)

                def rest():
                    for n in range(3, 6):
                        stage(n)
                    sp.wait_ge(g["w_lo_done"], 5)
                    sp.dma_start(we_in[0][:, 0:2 * D], w_kv).then_inc(g["w0_stage"], 16)
                    sp.dma_start(w_gate_sb[:], w_gate).then_inc(g["w_rest_in"], 16)
                    sp.dma_start(list_dram.rearrange("(a b) c -> a (b c)", a=P),
                                 list_fill).then_inc(g["dump_out"], 16)
                    sp.wait_ge(g["zeroed"], 1)
                    for t in (h_dram, out):
                        sp.dma_start(t[TOKENS:].rearrange("(p s) d -> p (s d)", p=P),
                                     zeros_sb[:]).then_inc(g["dump_out"], 16)

                def step(i, ahead, own, cross, tail, ranks):
                    if ahead:
                        after(sp, xn_done["s"], i + 1)
                        sp.dma_start(x_in[:], of(x, i + 1)).then_inc(g["x_in_s"], 16)
                    if isinstance(i, int) and i == -1:
                        stage(0)
                        for dst, src in ((bias_sb, biases), (rope_sb, rope)):
                            sp.dma_start(dst[:], src).then_inc(g["consts_in"], 16)
                        stage(1)
                        for dst, src in ((identb_sb, identb), (causal_sb, causal),
                                         (upper_sb, upper), (onesb_sb, onesb), (iota_e_sb, iota_e),
                                         (rows0_sb, list_rows0), (iota_p_sb, iota_p)):
                            sp.dma_start(dst[:], src).then_inc(g["consts_in"], 16)
                        stage(2)
                    if own:
                        after(sp, g["ctx_done"], i)
                        sp.dma_start(ctx_in[:], of(ctxT, i)).then_inc(g["ctx_in_s"], 16)
                        after(sp, g["resid_done"], i)
                        sp.dma_start(x_res[:], of(x, i)).then_inc(g["x_res_in"], 16)
                    if tail:
                        rows = slice((i - 2) * P, (i - 1) * P) if isinstance(i, int) else bass.ds((i - 2) * P, P)
                        sp.wait_ge(g["x2_done"], i - 1)
                        sp.dma_start(out[rows, :], x2[:]).then_inc(g["x2_out"], 16)
                        sp.wait_ge(xn_done["h"], i - 1)
                        sp.dma_start(h_dram[rows, :], xn["h"][:]).then_inc(g["h_out"], 16)

                run_steps(sp, step, rest)

                sp.wait_ge(m["tab_link"], 13)
                sp.dma_start(tab_dram, tab[:]).then_inc(m["tab_out"], 16)
                sp.wait_ge(m["tab_out"], 16)
                sp.dma_start(tab_row[:], tab_dram.rearrange("(o p) c -> o (p c)", o=1)).then_inc(m["tab_in"], 16)
                sp.wait_ge(m["tab_in"], 16)
                for u in range(2):
                    load_weights(sp, u, u)

            @block.tensor
            def _(pe):
                def transposes(dst, src, done):
                    for c in range(KC):
                        mm = nc.tensor.transpose(dst[:, c * P:(c + 1) * P], src[:, c * P:(c + 1) * P], ident_sb[:])
                    mm.then_inc(done, 1)

                def product(dst, lhsT, n, i):
                    c, (a, b) = i // len(PARTS), PARTS[i % len(PARTS)]
                    return nc.tensor.matmul(dst[:], lhsT(a)[:, c], w[n, b][:, c], start=(i == 0),
                                            stop=(i == PRODUCTS - 1), skip_group_check=True)

                def project(dst, lhsT, n):
                    for i in range(PRODUCTS):
                        mm = product(dst, lhsT, n, i)
                    return mm

                def mask():
                    for r in range(4):
                        nc.tensor.matmul(S[:, r], identb_sb[:], causal_sb[:], start=True, stop=False,
                                         skip_group_check=True)

                def scores(c, between):
                    for k in range(KC):
                        for n, (a, b) in enumerate(PARTS):
                            for r in range(4):
                                rows = slice(HD * r, HD * (r + 1))
                                if n == 0:
                                    between(4 * k + r)
                                mm = nc.tensor.matmul(S[:, r, k * TOK:(k + 1) * TOK], qT[c, a][rows, k],
                                                      kT[c, b][rows, k], start=(c == "s" and n == 0),
                                                      stop=(n == len(PARTS) - 1), skip_group_check=True)
                    mm.then_inc(scores_mm[c], 1)

                def probs_T(c, j, rs):
                    for r in rs:
                        pe.wait_ge(exp_done[c], HEADS * j + 4 * (r + 1))
                        if c == "s" and r == 3:
                            pe.wait_ge(pT_dve[c], 2 * j + 1)
                        for k in range(KC):
                            mm = nc.tensor.transpose(PT_BANK[c][r][:, k * P:(k + 1) * P], probs[c][:, 4 * r + k], ident_sb[:])
                        mm.then_inc(pT_tr[c], 1)

                def weighted_v(c, j, between):
                    pe.wait_ge(pT_act[c], 2 * (j + 1))
                    pe.wait_ge(pT_dve[c], 2 * (j + 1))
                    pe.wait_ge(v_done[c], j + 1)
                    for k in range(KC):
                        for r in range(4):
                            h = 4 * k + r
                            between(h)
                            mm = nc.tensor.matmul(T[0][:, h * HD:(h + 1) * HD], pT[c][:, 4 * r + k],
                                                  v[c][:, h * HD:(h + 1) * HD], start=True, stop=True)
                    mm.then_inc(pv_mm[c], 1)

                pe.wait_ge(g["ident_in"], 16)

                def step(i, ahead, own, cross, tail, ranks):
                    alone = isinstance(i, int)
                    if own:
                        pe.wait_ge(qT_done["s"], i + 1)
                        pe.wait_ge(kT_done["s"], i + 1)
                        after(pe, exp_done["x"], HEADS * (i - 1))
                        after(pe, pT_act["x"], 2 * (i - 1) - 1)
                        if alone and i == 0:
                            pe.wait_ge(g["w_lo_done"], 3)

                        def v_s(h):
                            if h % 4:
                                n = h // 4 * 3 + h % 4 - 1
                                mm = product(A, lambda p: xnT["s", p], 2, n)
                                if n == PRODUCTS - 1:
                                    mm.then_inc(g["v_mm"], 1)

                        scores("s", v_s)
                    if ahead:
                        pe.wait_ge(xn_done["s"], i + 2)
                        after(pe, pT_dve["x"], 2 * (i - 1))
                        transposes(T[1], xn["s"], xnT_tr["s"])
                    def rank():
                        pe.wait_ge(g["route_link"], ROUTE_LINKS * (i - 3) + 8)
                        nc.tensor.matmul(B[:, 0:EXPERTS], upper_sb[:], chosen[:], start=True, stop=False)
                        nc.tensor.matmul(B[:, 0:EXPERTS], onesb_sb[:], chosen_cum[:], start=False, stop=True
                                         ).then_inc(g["rank_mm"], 1)

                    def k_x(n):
                        if n == 0:
                            if alone and i == 1:
                                pe.wait_ge(g["w_lo_done"], 7)
                            pe.wait_ge(g["ctx_done"], i)
                            if own:
                                pe.wait_ge(v_done["s"], i + 1)
                        c, (a, b) = n // len(PARTS), PARTS[n % len(PARTS)]
                        mm = nc.tensor.matmul(A[:, c * P:(c + 1) * P], w_kv_p[a][:, c * P:(c + 1) * P], ctx_p[b][:],
                                              start=(n % len(PARTS) == 0), stop=(n % len(PARTS) == len(PARTS) - 1))
                        if n == PRODUCTS - 1:
                            mm.then_inc(g["kx_mm"], 1)

                    if ranks and not cross:
                        pe.wait_ge(pT_dve["x"], 2 * SEQS)
                        rank()
                    if tail:
                        def between(h):
                            if ranks and own and h == 7:
                                pe.wait_ge(pT_dve["x"], 2 * (i - 1))
                                rank()
                            if cross and h >= HEADS - PRODUCTS:
                                k_x(h - HEADS + PRODUCTS)

                        weighted_v("x", i - 2, between)
                    elif cross:
                        for n in range(PRODUCTS):
                            k_x(n)
                    if cross:
                        if own and ranks:
                            pe.wait_ge(g["route_link"], ROUTE_LINKS * (i - 3) + 10)
                        if not own:
                            pe.wait_ge(pT_dve["x"], 2 * (i - 1))
                        for n, (a, b) in enumerate(PARTS):
                            mm = nc.tensor.matmul(B[:], ctx_p[a][:], w_kv_p[b][:, D:], start=(n == 0),
                                                  stop=(n == len(PARTS) - 1))
                        mm.then_inc(g["vx_mm"], 1)

                    def k_s(ns):
                        for n in ns:
                            mm = product(T[1], lambda p: xnT["s", p], 1, n)
                        if n == PRODUCTS - 1:
                            mm.then_inc(g["k_mm"], 1)

                    first = 2 * PRODUCTS // 3
                    if ahead:
                        if alone and i == -1:
                            pe.wait_ge(g["w_lo_done"], 2)
                        pe.wait_ge(xnT_done["s"], i + 2)
                        k_s(range(first))
                    if tail:
                        pe.wait_ge(o_done["x"], i - 1)
                        if cross:
                            pe.wait_ge(v_done["x"], i)
                        elif ranks:
                            pe.wait_ge(g["route_link"], ROUTE_LINKS * (i - 3) + 10)
                        transposes(B, o["x"], oT_tr["x"])
                    if cross:
                        pe.wait_ge(xn_done["x"], i)
                        pe.wait_ge(kT_done["x"], i)
                        transposes(A, xn["x"], xnT_tr["x"])
                    if ranks and cross and not own:
                        pe.wait_ge(oT_done["x"], i - 1)
                        rank()
                    if ahead:
                        k_s(range(first, PRODUCTS))
                    if cross:
                        pe.wait_ge(xnT_done["x"], i)
                        for f in range(KC):
                            for c in range(KC):
                                for n, (a, b) in enumerate(PARTS):
                                    mm = nc.tensor.matmul(A[:, f * P:(f + 1) * P], w[4, a][:, c, f * P:(f + 1) * P],
                                                          xnT["x", b][:, c], start=(c == 0 and n == 0),
                                                          stop=(c == KC - 1 and n == len(PARTS) - 1))
                        mm.then_inc(g["qx_mm"], 1)
                    if own:
                        after(pe, g["x1_done"], i)
                        if ahead:
                            pe.wait_ge(g["k_done"], i + 2)
                        probs_T("s", i, (0, 1))
                    if cross:
                        if own:
                            pe.wait_ge(exp_done["s"], HEADS * (i + 1))
                        after(pe, exp_done["x"], HEADS * (i - 1))
                        mask()
                    if own:
                        if tail:
                            pe.wait_ge(oT_done["x"], i - 1)
                        elif cross:
                            pe.wait_ge(v_done["x"], i)
                        probs_T("s", i, (2, 3))
                    def w_out(n):
                        if n < PRODUCTS:
                            mm = product(T[0], lambda p: oT["x", p], 5, n)
                            if n == PRODUCTS - 1:
                                mm.then_inc(wo_mm["x"], 1)

                    if tail:
                        if alone and i == 2:
                            pe.wait_ge(g["w_rest_in"], 16)
                            pe.wait_ge(g["consts_in"], 16 * 9)
                        pe.wait_ge(oT_done["x"], i - 1)
                        if own:
                            pe.wait_ge(pT_act["s"], 2 * i + 1)
                    if cross:
                        pe.wait_ge(qT_done["x"], i)
                        scores("x", w_out if tail else lambda n: None)
                    elif tail:
                        for n in range(PRODUCTS):
                            w_out(n)

                    def q_s(n):
                        if n < PRODUCTS:
                            mm = product(B, lambda p: xnT["s", p], 0, n)
                            if n == PRODUCTS - 1:
                                mm.then_inc(g["q_mm"], 1)

                    first_q = PRODUCTS if not own else len(PARTS)
                    if ahead:
                        if own:
                            pe.wait_ge(pT_act["s"], 2 * (i + 1))
                        else:
                            pe.wait_ge(g["k_done"], i + 2)
                        for n in range(first_q):
                            q_s(n)
                    if own:
                        if tail:
                            pe.wait_ge(g["x2_done"], i - 1)
                        weighted_v("s", i, (lambda h: q_s(first_q + h)) if ahead else lambda h: None)
                    if tail:
                        pe.wait_ge(xn_done["h"], i - 1)
                        transposes(A, xn["h"], xnT_tr["h"])
                    if ahead:
                        pe.wait_ge(g["q_done"], i + 2)
                        pe.wait_ge(g["rope_done"], 2 * (i + 1) + 1)
                        transposes(B, qk_r[:, 1], g["kT_tr"])
                    if own:
                        pe.wait_ge(o_done["s"], i + 1)
                        transposes(T[1], o["s"], oT_tr["s"])
                        if alone and i == 0:
                            pe.wait_ge(g["w_lo_done"], 4)
                    if tail:
                        pe.wait_ge(xnT_done["h"], i - 1)
                        for c in range(KC):
                            mm = nc.tensor.matmul(A[:, 0:EXPERTS], hT[:, c], w_gate_sb[:, c],
                                                  start=(c == 0), stop=(c == KC - 1))
                        mm.then_inc(g["logits_mm"], 1)
                    if own:
                        pe.wait_ge(oT_done["s"], i + 1)
                        project(T[0], lambda p: oT["s", p], 3).then_inc(wo_mm["s"], 1)
                    if ahead:
                        pe.wait_ge(g["rope_done"], 2 * (i + 2))
                        transposes(T[1], qk_r[:, 0], g["qT_tr"])
                    if cross:
                        if tail:
                            pe.wait_ge(g["ex_done"], i - 1)
                        if ahead:
                            pe.wait_ge(kT_done["s"], i + 2)
                        elif own:
                            pe.wait_ge(pT_act["s"], 2 * (i + 1))
                        else:
                            pe.wait_ge(g["route_link"], ROUTE_LINKS * (i - 3) + 10)
                        probs_T("x", i - 1, (0, 1))
                        if own:
                            pe.wait_ge(g["x1_done"], i + 1)
                        else:
                            pe.wait_ge(g["x2_done"], i - 1)
                        probs_T("x", i - 1, (2,))
                        if ahead:
                            pe.wait_ge(qT_done["s"], i + 2)
                        probs_T("x", i - 1, (3,))

                run_steps(pe, step)

                pe.wait_ge(g["route_link"], ROUTE_LINKS * (SEQS - 1) + 9)
                pe.wait_ge(g["ex_done"], SEQS)
                nc.tensor.matmul(A[:, 0:EXPERTS], onesb_sb[:], chosen_cum[:], start=True, stop=True
                                 ).then_inc(m["cum_mm"], 1)

            @block.scalar
            def _(act):
                def split_weights(ns):
                    for n in ns:
                        act.wait_ge(g[f"w{n % 2}_stage"], 16 * (n // 2 + 1))
                        nc.scalar.mul(flat(w[n, "hi"]), we_in[n % 2][:, 0:KC * D], W_SCALE).then_inc(g["w_hi_done"], 1)

                def split_rest():
                    split_weights(range(3, 6))
                    act.wait_ge(g["w0_stage"], 16 * 4)
                    nc.scalar.mul(w_kv_p["hi"][:], we_in[0][:, 0:2 * D], W_SCALE).then_inc(g["w_hi_done"], 1)

                def exps(c, j, rs):
                    after(act, pT_tr[c], 4 * j)
                    after(act, rinv_done[c], j)
                    for r in rs:
                        act.wait_ge(nmax_done[c], 4 * j + r + 1)
                        for k in range(KC):
                            n = 4 * r + k
                            nc.scalar.activation(probs[c][:, n], S[:, r, k * TOK:(k + 1) * TOK], ACT.Exp,
                                                 bias=nmax[c][:, n:n + 1],
                                                 accum_out=rsum[c][:, n:n + 1]).then_inc(exp_done[c], 1)

                def qT_high(c, j, src, scale):
                    after(act, scores_mm[c], j)
                    nc.scalar.mul(flat(qT[c, "hi"]), src[:], scale).then_inc(qT_hi[c], 1)

                def kT_high(c, j, src, scale):
                    after(act, scores_mm[c], j)
                    nc.scalar.mul(flat(kT[c, "hi"]), src[:], scale).then_inc(kT_hi[c], 1)

                def pT_copy(c, j, r):
                    after(act, pv_mm[c], j)
                    act.wait_ge(pT_tr[c], 4 * j + r + 1)
                    nc.scalar.copy(pT[c][:, 4 * r:4 * r + 4].rearrange("p h t -> p (h t)"), PT_BANK[c][r][:]
                                   ).then_inc(pT_act[c], 1)

                def oT_high(c, j, src):
                    act.wait_ge(oT_tr[c], j + 1)
                    after(act, wo_mm[c], j)
                    nc.scalar.copy(flat(oT[c, "hi"]), src[:]).then_inc(oT_hi[c], 1)

                def xnT_high(c, j, src, used):
                    act.wait_ge(xnT_tr[c], j + 1)
                    after(act, used, j)
                    nc.scalar.copy(flat(xnT[c, "hi"]), src[:]).then_inc(xnT_hi[c], 1)

                split_weights(range(2))

                def step(i, ahead, own, cross, tail, ranks):
                    if ahead:
                        xnT_high("s", i + 1, T[1], g["v_mm"])
                    if isinstance(i, int) and i == -1:
                        split_weights([2])
                    if own:
                        exps("s", i, (0, 1))
                    if cross:
                        act.wait_ge(g["kx_mm"], i)
                        kT_high("x", i - 1, A, 1.0 / W_SCALE)
                    if cross:
                        xnT_high("x", i - 1, A, g["qx_mm"])
                    if tail:
                        oT_high("x", i - 2, B)
                    if own:
                        exps("s", i, (2, 3))
                    if cross:
                        act.wait_ge(g["qx_mm"], i)
                        qT_high("x", i - 1, A, INV_SQRT_HD / W_SCALE)
                    if own:
                        pT_copy("s", i, 0)
                        pT_copy("s", i, 2)
                    if cross:
                        exps("x", i - 1, range(4))
                    if own:
                        oT_high("s", i, T[1])
                    if ahead:
                        act.wait_ge(g["kT_tr"], i + 2)
                        kT_high("s", i + 1, B, 1.0)
                    if tail:
                        act.wait_ge(g["lmax_done"], i - 1)
                        after(act, g["route_link"], ROUTE_LINKS * (i - 3) + 2)
                        nc.scalar.activation(gate_e[:], A[:, 0:EXPERTS], ACT.Exp, bias=lmax[:]
                                             ).then_inc(g["ex_done"], 1)
                    if ahead:
                        act.wait_ge(g["qT_tr"], i + 2)
                        qT_high("s", i + 1, T[1], INV_SQRT_HD)
                    if cross:
                        pT_copy("x", i - 1, 0)
                        pT_copy("x", i - 1, 2)

                run_steps(act, step, split_rest)

            @block.vector
            def _(dve):
                def split_weights(ns):
                    for n in ns:
                        dve.wait_ge(g["w_hi_done"], n + 1)
                        nc.vector.scalar_tensor_tensor(flat(w[n, "lo"]), we_in[n % 2][:, 0:KC * D], W_SCALE,
                                                       flat(w[n, "hi"]), ALU.mult, ALU.subtract
                                                       ).then_inc(g["w_lo_done"], 1)

                def split_rest():
                    split_weights(range(3, 6))
                    dve.wait_ge(g["w_hi_done"], 7)
                    nc.vector.scalar_tensor_tensor(w_kv_p["lo"][:], we_in[0][:, 0:2 * D], W_SCALE,
                                                   w_kv_p["hi"][:], ALU.mult, ALU.subtract
                                                   ).then_inc(g["w_lo_done"], 1)

                def norm_stats(c, j, src):
                    nc.vector.bn_stats(stats[c][:], src[:]).then_inc(stats_done[c], 1)
                    dve.wait_ge(stats_done[c], j + 1)
                    apart(dve)
                    nc.vector.bn_aggr(mv[c][:], stats[c][:]).then_inc(mv_done[c], 1)

                def normalise(c, j, src):
                    dve.wait_ge(rstd_done[c], j + 1)
                    nc.vector.tensor_scalar(xn[c][:], src[:], mv[c][:, 0:1], rstd[c][:], ALU.subtract,
                                            ALU.mult).then_inc(xn_done[c], 1)

                def row_max(c, j, r):
                    dve.wait_ge(scores_mm[c], j + 1)
                    after(dve, exp_done[c], HEADS * j)
                    nc.vector.tensor_reduce(nmax[c][:, 4 * r:4 * r + 4], S[:, r].rearrange("p (k t) -> p k t", k=KC),
                                            AX_X, ALU.max, negate=True).then_inc(nmax_done[c], 1)

                def invert_sums(c, j):
                    dve.wait_ge(exp_done[c], HEADS * (j + 1))
                    nc.vector.reciprocal(rinv[c][:], rsum[c][:]).then_inc(rinv_done[c], 1)

                def pT_copy(c, j, r):
                    after(dve, pv_mm[c], j)
                    dve.wait_ge(pT_tr[c], 4 * j + r + 1)
                    nc.vector.tensor_copy(pT[c][:, 4 * r:4 * r + 4].rearrange("p h t -> p (h t)"), PT_BANK[c][r][:]
                                          ).then_inc(pT_dve[c], 1)

                def scale_out(c, j):
                    dve.wait_ge(pv_mm[c], j + 1)
                    dve.wait_ge(rinv_done[c], j + 1)
                    after(dve, oT_tr[c], j)
                    nc.vector.tensor_tensor(
                        o[c][:].rearrange("p (k r d) -> p k r d", k=KC, r=4),
                        T[0][:].rearrange("p (k r d) -> p k r d", k=KC, r=4),
                        rinv[c][:].rearrange("p (r k) -> p k r", r=4).unsqueeze(3).to_broadcast([P, KC, 4, HD]),
                        ALU.mult).then_inc(o_done[c], 1)

                def oT_low(c, j, src):
                    dve.wait_ge(oT_hi[c], j + 1)
                    after(dve, wo_mm[c], j)
                    nc.vector.tensor_tensor(flat(oT[c, "lo"]), src[:], flat(oT[c, "hi"]), ALU.subtract
                                            ).then_inc(oT_done[c], 1)

                def xnT_low(c, j, src, used):
                    dve.wait_ge(xnT_hi[c], j + 1)
                    after(dve, used, j)
                    nc.vector.tensor_tensor(flat(xnT[c, "lo"]), src[:], flat(xnT[c, "hi"]), ALU.subtract
                                            ).then_inc(xnT_done[c], 1)

                def qT_low(c, j, src, scale):
                    dve.wait_ge(qT_hi[c], j + 1)
                    after(dve, scores_mm[c], j)
                    nc.vector.scalar_tensor_tensor(flat(qT[c, "lo"]), src[:], scale, flat(qT[c, "hi"]), ALU.mult,
                                                   ALU.subtract).then_inc(qT_done[c], 1)

                def kT_low(c, j, src, scale):
                    dve.wait_ge(kT_hi[c], j + 1)
                    after(dve, scores_mm[c], j)
                    nc.vector.scalar_tensor_tensor(flat(kT[c, "lo"]), src[:], scale, flat(kT[c, "hi"]), ALU.mult,
                                                   ALU.subtract).then_inc(kT_done[c], 1)

                def unscaled_plus(dst, src, other):
                    return nc.vector.scalar_tensor_tensor(dst, src[:], 1.0 / W_SCALE, other, ALU.mult, ALU.add)

                def rotate_cos(a):
                    return nc.vector.tensor_tensor(
                        rope_c[:, a].rearrange("p (h d) -> p h d", d=HD), qk[:, a].rearrange("p (h d) -> p h d", d=HD),
                        rope_sb[:, 0].unsqueeze(1).to_broadcast([P, HEADS, HD]), ALU.mult
                    ).then_inc(g["rope_c_done"], 1)

                def rotated(a, j):
                    n = 2 * j + (1 if a else 2)
                    dve.wait_ge(g["rope_c_done"], n)
                    dve.wait_ge(g["rope_s_done"], 2 * n)
                    after(dve, g["kT_tr" if a else "qT_tr"], j)
                    nc.vector.tensor_tensor(qk_r[:, a], rope_c[:, a], rope_s[:, a], ALU.add).then_inc(g["rope_done"], 1)

                def link(j, n, ins):
                    ins.then_inc(g["route_link"], 1)
                    dve.wait_ge(g["route_link"], ROUTE_LINKS * j + n)

                nc.vector.memset(zeros_sb[:], 0.0).then_inc(g["zeroed"], 1)
                nc.vector.memset(chosen_cum[:], 0.0).then_inc(g["cum_zero"], 1)

                def step(i, ahead, own, cross, tail, ranks):
                    j = i - 3
                    if ahead:
                        dve.wait_ge(g["x_in_s"], 16 * (i + 2))
                        norm_stats("s", i + 1, x_in)
                    if ranks:
                        dve.wait_ge(g["ex_done"], i - 2)
                        after(dve, g["list_out"], 16 * TOP_K * (i - 3))
                        apart(dve)
                        link(j, 1, nc.vector.max(top_v[:], gate_e[:]))
                        apart(dve)
                        link(j, 2, nc.vector.max_index(top_i[:], top_v[:], gate_e[:]))
                        link(j, 3, nc.vector.tensor_reduce(top_s[:], top_v[:], AX_X, ALU.add))
                        link(j, 4, nc.vector.reciprocal(top_r[:], top_s[:]))
                        link(j, 5, nc.vector.tensor_scalar(rec[:].bitcast(F32)[:, :, 1], top_v[:], top_r[:],
                                                           1.0 / W_SCALE, ALU.mult, ALU.mult))
                        link(j, 6, nc.vector.tensor_copy(top_f[:], top_i[:]))
                    if ahead:
                        after(dve, xnT_tr["s"], i + 1)
                        normalise("s", i + 1, x_in)
                    if isinstance(i, int) and i == -1:
                        split_weights(range(2))
                    if own:
                        dve.wait_ge(g["v_mm"], i + 1)
                        after(dve, pv_mm["s"], i)
                        unscaled_plus(v["s"][:], A, bias_sb[:, 2]).then_inc(v_done["s"], 1)
                        row_max("s", i, 0)

                    def ranked():
                        dve.wait_ge(g["rank_mm"], i - 2)
                        link(j, 9, nc.vector.tensor_tensor(chosen_cum[:], chosen_cum[:], chosen[:], ALU.add))
                        link(j, 10, nc.vector.tensor_tensor(row_of[:], B[:, 0:EXPERTS], rows0_sb[:], ALU.add))

                    def list_rows():
                        link(j, 11, nc.vector.tensor_tensor(
                            row_sel[:], onehot[:], row_of[:].unsqueeze(1).to_broadcast([P, TOP_K, EXPERTS]),
                            ALU.mult))
                        link(j, 12, nc.vector.tensor_reduce(pos_f[:], row_sel[:], AX_X, ALU.add))
                        link(j, 13, nc.vector.tensor_copy(pos_u[:], pos_f[:]))

                    if ranks:
                        link(j, 7, nc.vector.tensor_tensor(
                            onehot[:], iota_e_sb[:].unsqueeze(1).to_broadcast([P, TOP_K, EXPERTS]),
                            top_f[:].unsqueeze(2).to_broadcast([P, TOP_K, EXPERTS]), ALU.is_equal))
                        with nc.allow_low_precision(reason="sums of zeros and ones are exact"):
                            link(j, 8, nc.vector.tensor_reduce(chosen[:], onehot[:].rearrange("p k e -> p e k"),
                                                               AX_X, ALU.add))
                    if own:
                        row_max("s", i, 1)
                    if ahead:
                        xnT_low("s", i + 1, T[1], g["v_mm"])
                    if own:
                        row_max("s", i, 2)
                    if ranks and own:
                        ranked()
                    if own:
                        row_max("s", i, 3)
                    if isinstance(i, int) and i == -1:
                        split_weights([2])
                        dve.wait_ge(g["consts_in"], 16 * 9)
                    if ranks and not cross:
                        ranked()
                        list_rows()
                    if tail:
                        invert_sums("x", i - 2)
                        scale_out("x", i - 2)
                    if cross:
                        dve.wait_ge(g["vx_mm"], i)
                        after(dve, pv_mm["x"], i - 1)
                        nc.vector.tensor_scalar(v["x"][:], B[:], 1.0 / W_SCALE, None, ALU.mult
                                                ).then_inc(v_done["x"], 1)
                        kT_low("x", i - 1, A, 1.0 / W_SCALE)
                    if cross:
                        xnT_low("x", i - 1, A, g["qx_mm"])
                    if tail:
                        oT_low("x", i - 2, B)
                    if ranks and cross:
                        if not own:
                            ranked()
                        list_rows()
                    if ahead:
                        dve.wait_ge(g["k_mm"], i + 2)
                        after(dve, g["rope_s_done"], 4 * (i + 1))
                        after(dve, g["rope_done"], 2 * (i + 1))
                        unscaled_plus(qk[:, 1], T[1], bias_sb[:, 1]).then_inc(g["k_done"], 1)
                        dve.wait_ge(g["k_done"], i + 2)
                        rotate_cos(1)
                    if own:
                        pT_copy("s", i, 1)
                    if cross:
                        qT_low("x", i - 1, A, INV_SQRT_HD / W_SCALE)
                    if own:
                        pT_copy("s", i, 3)
                        invert_sums("s", i)
                    if ahead:
                        rotated(1, i + 1)
                    if tail:
                        dve.wait_ge(wo_mm["x"], i - 1)
                        dve.wait_ge(g["held_done"], i - 1)
                        after(dve, g["x2_out"], 16 * (i - 2))
                        unscaled_plus(x2[:], T[0], x1_held[:]).then_inc(g["x2_done"], 1)
                    if cross:
                        row_max("x", i - 1, 0)
                    if tail:
                        dve.wait_ge(g["x2_done"], i - 1)
                        norm_stats("h", i - 2, x2)
                    if cross:
                        for r in range(1, 4):
                            row_max("x", i - 1, r)
                    if tail:
                        after(dve, xnT_tr["h"], i - 2)
                        after(dve, g["h_out"], 16 * (i - 2))
                        normalise("h", i - 2, x2)
                    if ahead:
                        dve.wait_ge(g["q_mm"], i + 2)
                        unscaled_plus(qk[:, 0], B, bias_sb[:, 0]).then_inc(g["q_done"], 1)
                    if own:
                        scale_out("s", i)
                    if tail:
                        dve.wait_ge(xnT_tr["h"], i - 1)
                        after(dve, g["logits_mm"], i - 2)
                        nc.vector.tensor_copy(flat(hT), A[:]).then_inc(xnT_done["h"], 1)
                    if own:
                        oT_low("s", i, T[1])
                    if ahead:
                        dve.wait_ge(g["q_done"], i + 2)
                        rotate_cos(0)
                    if tail:
                        dve.wait_ge(g["logits_mm"], i - 1)
                        after(dve, g["ex_done"], i - 2)
                        nc.vector.tensor_reduce(lmax[:], A[:, 0:EXPERTS], AX_X, ALU.max, negate=True
                                                ).then_inc(g["lmax_done"], 1)
                    if ahead:
                        rotated(0, i + 1)
                        kT_low("s", i + 1, B, 1.0)
                    if own:
                        dve.wait_ge(wo_mm["s"], i + 1)
                        dve.wait_ge(g["resid_done"], i + 1)
                        after(dve, g["held_done"], i)
                        unscaled_plus(x1[:], T[0], resid[:]).then_inc(g["x1_done"], 1)
                    if ahead:
                        qT_low("s", i + 1, T[1], INV_SQRT_HD)
                    if own:
                        dve.wait_ge(g["x1_done"], i + 1)
                        norm_stats("x", i, x1)
                    if cross:
                        pT_copy("x", i - 1, 1)
                    if own:
                        after(dve, xnT_tr["x"], i)
                        normalise("x", i, x1)
                    if cross:
                        pT_copy("x", i - 1, 3)

                run_steps(dve, step, split_rest)

                def tab_link(n, ins):
                    ins.then_inc(m["tab_link"], 1)
                    dve.wait_ge(m["tab_link"], n)

                dve.wait_ge(m["cum_mm"], 1)
                tab_link(1, nc.vector.tensor_scalar(cnt[:], A[:, 0:EXPERTS], float(TILE - 1), None, ALU.add))
                tab_link(2, nc.vector.tensor_copy(cnt_i[:], cnt[:]))
                tab_link(3, nc.vector.tensor_scalar(cnt_s[:], cnt_i[:], TILE.bit_length() - 1, None,
                                                ALU.arith_shift_right))
                tab_link(4, nc.vector.tensor_copy(ntile[:], cnt_s[:]))
                tab_link(5, nc.vector.tensor_tensor_scan(ncum[:], zeros_sb[:, 0:EXPERTS], ntile[:], 0.0, ALU.add, ALU.add))
                tab_link(6, nc.vector.tensor_scalar(passed[:], ncum[:], iota_p_sb[:], None, ALU.is_le))
                tab_link(7, nc.vector.tensor_tensor(passed_n[:], passed[:], ntile[:], ALU.mult))
                tab_link(8, nc.vector.tensor_reduce(tab_e[:], passed[:], AX_X, ALU.add))
                tab_link(9, nc.vector.tensor_reduce(tab_a[:], passed_n[:], AX_X, ALU.add))
                tab_link(10, nc.vector.tensor_scalar(tab_b[:], tab_a[:], iota_p_sb[:], -float(TILE), ALU.subtract, ALU.mult))
                tab_link(11, nc.vector.scalar_tensor_tensor(tab_c[:], tab_e[:], float(TOKENS), tab_b[:], ALU.mult, ALU.add))
                tab_link(12, nc.vector.tensor_scalar(tab[:, 1:2], tab_c[:], float(EXPERTS * TOKENS), None, ALU.min))
                tab_link(13, nc.vector.tensor_scalar(tab[:, 0:1], tab_e[:], float(EXPERTS - 1), None, ALU.min))

            @block.gpsimd
            def _(pool):
                nc.gpsimd.memset(half_sb[:], -0.5).then_inc(g["half_set"], 1)
                pool.wait_ge(g["half_set"], 1)

                def inv_std(c, j):
                    pool.wait_ge(mv_done[c], j + 1)
                    apart(pool)
                    nc.gpsimd.tensor_scalar(vare[c][:], mv[c][:, 1:2], EPS, None, ALU.add).then_inc(vare_done[c], 1)
                    pool.wait_ge(vare_done[c], j + 1)
                    nc.gpsimd.tensor_tensor(rstd[c][:], vare[c][:], half_sb[:], ALU.pow).then_inc(rstd_done[c], 1)

                def rotate_sin(a, j):
                    pool.wait_ge(g["k_done" if a else "q_done"], j + 1)
                    src = qk[:, a].rearrange("p (h s d) -> p h s d", s=2, d=HD // 2)
                    dst = rope_s[:, a].rearrange("p (h s d) -> p h s d", s=2, d=HD // 2)
                    sin = rope_sb[:, 1].rearrange("p (s d) -> p s d", s=2)
                    for s in range(2):
                        nc.gpsimd.tensor_tensor(
                            dst[:, :, s], src[:, :, 1 - s],
                            sin[:, s].unsqueeze(1).to_broadcast([P, HEADS, HD // 2]), ALU.mult
                        ).then_inc(g["rope_s_done"], 1)

                def step(i, ahead, own, cross, tail, ranks):
                    if ahead:
                        inv_std("s", i + 1)
                    if isinstance(i, int) and i == -1:
                        pool.wait_ge(g["consts_in"], 16 * 9)
                        nc.gpsimd.tensor_copy(tok_f[:], iota_p_sb[:]).then_inc(g["tok_adv"], 1)
                    if own:
                        pool.wait_ge(g["ctx_in_s"], 16 * (i + 1))
                        after(pool, g["vx_mm"], i)
                        apart(pool)
                        nc.gpsimd.tensor_copy(ctx_p["hi"][:], ctx_in[:]).then_inc(g["ctx_hi"], 1)
                        pool.wait_ge(g["ctx_hi"], i + 1)
                        nc.gpsimd.tensor_tensor(ctx_p["lo"][:], ctx_in[:], ctx_p["hi"][:], ALU.subtract
                                                ).then_inc(g["ctx_done"], 1)
                    if ahead:
                        after(pool, g["rope_done"], 2 * (i + 1))
                        rotate_sin(1, i + 1)
                    if ranks:
                        j = i - 3
                        if isinstance(i, int) and i == 3:
                            pool.wait_ge(g["dump_out"], 16 * 3)
                        after(pool, g["list_out"], 16 * TOP_K * (i - 3))
                        pool.wait_ge(g["tok_adv"], i - 2)
                        apart(pool)
                        nc.gpsimd.tensor_copy(rec[:, :, 0], tok_f[:].to_broadcast([P, TOP_K])
                                              ).then_inc(g["rec_tok"], 1)
                        pool.wait_ge(g["rec_tok"], i - 2)
                        apart(pool)
                        nc.gpsimd.tensor_scalar(tok_f[:], tok_f[:], float(TOK), None, ALU.add
                                                ).then_inc(g["tok_adv"], 1)
                        pool.wait_ge(g["route_link"], ROUTE_LINKS * j + 13)
                        apart(pool)
                        for k in range(TOP_K):
                            pool.indirect_dma_start(
                                out=list_dram[:, :], out_offset=bass.IndirectOffsetOnAxis(ap=pos_u[:, k:k + 1], axis=0),
                                in_=rec[:, k, :], in_offset=None).then_inc(g["list_out"], 16)
                    if tail:
                        inv_std("h", i - 2)
                    if cross:
                        pool.wait_ge(g["x1_done"], i)
                        after(pool, g["x2_done"], i - 1)
                        apart(pool)
                        nc.gpsimd.tensor_copy(x1_held[:], x1[:]).then_inc(g["held_done"], 1)
                    if own:
                        pool.wait_ge(g["x_res_in"], 16 * (i + 1))
                        after(pool, g["x1_done"], i)
                        nc.gpsimd.tensor_tensor(resid[:], x_res[:], bias_sb[:, 3], ALU.add
                                                ).then_inc(g["resid_done"], 1)
                    if ahead:
                        rotate_sin(0, i + 1)
                    if own:
                        inv_std("x", i)

                run_steps(pool, step)

        we_in += [sb(f"we_in{s}", [P, W_COLS]) for s in range(2, ROW_AHEAD)]
        we.update({(n, s): sb(f"we_{n}{s}", [P, W_COLS], F16) for n in ("hi", "lo") for s in range(2, ROW_AHEAD)})
        lst = [sb(f"lst{s}", [P, SUBS, 2], U32) for s in range(RING)]
        xg = [sb(f"xg{s}", [P, SUBS, D]) for s in range(ROW_AHEAD)]
        xgT = {(n, s): sb(f"xgT_{n}{s}", [P, KC, TILE], F16) for n in ("hi", "lo") for s in range(2)}
        silu_a = sb("silu_a", [P, TILE])
        silu_b = sb("silu_b", [MB, TILE])
        mid_a = sb("mid_a", [P, TILE])
        mid_b = sb("mid_b", [MB, TILE])
        ma = {n: sb(f"ma_{n}", [P, TILE], F16) for n in ("hi", "lo")}
        mb = sb("mb", [P, TILE], F16)
        y = [sb(f"y{s}", [P, SUBS, D]) for s in range(2)]
        GU = ((S[:, 2], S[:, 3]), (A, B))

        block2 = ctx.enter_context(nc.Block())
        GROUPS = -(-MOE_TILES // RING)

        def run_tiles(eng, tile):
            for u in range(RING):
                tile(u, u, 0, RING)
            with eng.Fori(1, GROUPS - 1) as n:
                for u in range(RING):
                    tile(n * RING + u, u, n, RING)
            for u in range(MOE_TILES - (GROUPS - 1) * RING):
                t = (GROUPS - 1) * RING + u
                tile(t, u, GROUPS - 1, MOE_TILES - 1 - t)

        @block2.sync
        def _(sp):
            sp.wait_ge(g["list_out"], 16 * TOP_K * SEQS)

            def load_list(t, u):
                r = sp.value_load(tab_row[0:1, bass.ds(2 * t + 1, 1)], min_val=0, max_val=LIST_ROWS - TILE)
                after(sp, m["added"], 16 * SUBS * (t - RING + 1))
                sp.dma_start(lst[u][:], list_dram[bass.ds(r, TILE), :].rearrange("(s p) c -> p s c", s=SUBS)
                             ).then_inc(m[f"l{u}_in"], 16)

            for u in range(LIST_AHEAD):
                load_list(u, u)
            sp.wait_ge(m["g1_in"], 16 * SUBS)
            for u in range(2, LOAD_AHEAD):
                load_weights(sp, u, u)

            def tile(t, u, n, left):
                if left >= LOAD_AHEAD:
                    load_weights(sp, t + LOAD_AHEAD, u + LOAD_AHEAD)
                if left >= LIST_AHEAD:
                    load_list(t + LIST_AHEAD, (u + LIST_AHEAD) % RING)

            run_tiles(sp, tile)
            sp.wait_ge(m["added"], 16 * SUBS * MOE_TILES)
            sp.wait_ge(g["x2_out"], 16 * SEQS)
            sp.wait_ge(g["h_out"], 16 * SEQS)

        @block2.gpsimd
        def _(pool):
            pool.wait_ge(g["h_out"], 16 * SEQS)
            pool.wait_ge(g["x2_out"], 16 * SEQS)

            def gather(t, u, n):
                after(pool, m["xT_mm"], 2 * (t - ROW_AHEAD + 1))
                pool.wait_ge(m[f"l{u}_in"], 16 * (n + 1))
                apart(pool)
                for q in range(SUBS):
                    pool.indirect_dma_start(
                        out=xg[u % ROW_AHEAD][:, q], out_offset=None, in_=h_dram[:, :],
                        in_offset=bass.IndirectOffsetOnAxis(ap=lst[u][:, q, 0:1], axis=0)
                    ).then_inc(m[f"g{u % ROW_AHEAD}_in"], 16)

            for u in range(ROW_AHEAD):
                gather(u, u, 0)

            def tile(t, u, n, left):
                if left >= ROW_AHEAD:
                    gather(t + ROW_AHEAD, (u + ROW_AHEAD) % RING, n + (u + ROW_AHEAD) // RING)
                after(pool, m["added"], 16 * SUBS * t)
                pool.wait_ge(m["y_act"], t + 1)
                pool.wait_ge(m["y_dve"], t + 1)
                apart(pool)
                for q in range(SUBS):
                    pool.indirect_dma_start(
                        out=out[:, :], out_offset=bass.IndirectOffsetOnAxis(ap=lst[u][:, q, 0:1], axis=0),
                        in_=y[u % 2][:, q], in_offset=None, compute_op=ALU.add).then_inc(m["added"], 16)

            run_tiles(pool, tile)

        @block2.tensor
        def _(pe):
            def turn(t, u, n):
                pe.wait_ge(m[f"g{u % ROW_AHEAD}_in"], 16 * SUBS * (RING // ROW_AHEAD * n + u // ROW_AHEAD + 1))
                for h in range(2):
                    after(pe, m["xT_lo_done"], 2 * (t - 1) + h + 1)
                    for k in (2 * h, 2 * h + 1):
                        for q in range(SUBS):
                            mm = nc.tensor.transpose(S[:, h, (k % 2) * TILE + q * P:(k % 2) * TILE + (q + 1) * P],
                                                     xg[u % ROW_AHEAD][:, q, k * P:(k + 1) * P], ident_sb[:])
                    mm.then_inc(m["xT_mm"], 1)

            def gate_up(t, u):
                first, second = GU[u % 2]
                pe.wait_ge(m["xT_lo_done"], 2 * (t + 1))
                pe.wait_ge(m["we_lo_done"], t + 1)
                after(pe, m["mid_done"], 2 * (t - 1))
                for c, dst in ((0, first[:, 0:TILE]), (1, first[:, TILE:2 * TILE]), (2, second[:, 0:TILE])):
                    for k in range(KC):
                        for i, (wn, xn_) in enumerate(PARTS):
                            w = we[wn, u % ROW_AHEAD][:, k * 2 * MID + c * P:k * 2 * MID + (c + 1) * P]
                            mm = nc.tensor.matmul(dst, w, xgT[xn_, u % 2][:, k], start=(k == 0 and i == 0),
                                                  stop=(k == KC - 1 and i == len(PARTS) - 1))
                    if c:
                        mm.then_inc(m["gu_mm"], 1)

            def down(t, u):
                first_rows, last_rows = slice(GU_COLS, GU_COLS + D), slice(GU_COLS + D, W_COLS)
                hi, lo = we["hi", u % ROW_AHEAD], we["lo", u % ROW_AHEAD]
                for q in range(SUBS):
                    after(pe, m["y_dve" if q else "y_act"], t)
                    cols = slice(q * P, (q + 1) * P)
                    pe.wait_ge(m["mid_lo_done"], 2 * t + 1)
                    for i, (mn, wn) in enumerate(PARTS):
                        nc.tensor.matmul(T[q][:], ma[mn][:, cols], we[wn, u % ROW_AHEAD][:, first_rows],
                                         start=(i == 0), stop=False)
                    pe.wait_ge(m["mid_lo_done"], 2 * t + 2)
                    nc.tensor.matmul(T[q][:], mb[:, cols], hi[:, last_rows], start=False, stop=False)
                    nc.tensor.matmul(T[q][:], mb[0:MB, cols], lo[0:MB, last_rows], start=False, stop=True
                                     ).then_inc(m["dn_mm"], 1)

            turn(0, 0, 0)
            gate_up(0, 0)
            turn(1, 1, 0)

            def tile(t, u, n, left):
                if left >= 2:
                    turn(t + 2, (u + 2) % RING, n + (u + 2) // RING)
                if left >= 1:
                    gate_up(t + 1, u + 1)
                down(t, u)

            run_tiles(pe, tile)

        @block2.scalar
        def _(act):
            def xT_hi(t, s):
                for h in range(2):
                    act.wait_ge(m["xT_mm"], 2 * t + h + 1)
                    after(act, m["gu_mm"], 2 * (t - 1))
                    nc.scalar.copy(xgT["hi", s][:, 2 * h:2 * h + 2].rearrange("p k t -> p (k t)"), S[:, h]
                                   ).then_inc(m["xT_hi_done"], 1)

            def weigh(t, u):
                act.wait_ge(m["dn_mm"], 2 * t + 1)
                after(act, m["added"], 16 * SUBS * (t - 1))
                nc.scalar.activation(y[u % 2][:, 0], T[0][:], ACT.Copy, scale=lst[u % RING][:].bitcast(F32)[:, 0, 1:2]
                                     ).then_inc(m["y_act"], 1)

            weights_hi(act, 0, 0, 0)
            weights_hi(act, 1, 1, 0)
            xT_hi(0, 0)
            xT_hi(1, 1)
            weights_hi(act, 2, 2, 0)

            def tile(t, u, n, left):
                first, second = GU[u % 2]
                for c, dst, src in ((1, silu_a, first[:, 0:TILE]), (2, silu_b, second[0:MB, 0:TILE])):
                    act.wait_ge(m["gu_mm"], 2 * t + c)
                    after(act, m["mid_done"], 2 * (t - 1) + c)
                    nc.scalar.activation(dst[:], src, ACT.Silu, scale=1.0 / W_SCALE).then_inc(m["silu_done"], 1)
                if not (isinstance(t, int) and t == 0):
                    weigh(t - 1, u - 1)
                if left >= 2:
                    xT_hi(t + 2, u % 2)
                for c, hi, src in ((1, ma["hi"][:], mid_a), (2, mb[0:MB], mid_b)):
                    act.wait_ge(m["mid_done"], 2 * t + c)
                    after(act, m["dn_mm"], SUBS * t)
                    nc.scalar.copy(hi, src[:]).then_inc(m["mid_hi_done"], 1)
                if left >= SPLIT_AHEAD:
                    weights_hi(act, t + SPLIT_AHEAD, (u + SPLIT_AHEAD) % RING, n + (u + SPLIT_AHEAD) // RING)

            run_tiles(act, tile)
            weigh(MOE_TILES - 1, (MOE_TILES - 1) % RING)

        @block2.vector
        def _(dve):
            def xT_lo(t, s):
                for h in range(2):
                    dve.wait_ge(m["xT_hi_done"], 2 * t + h + 1)
                    after(dve, m["gu_mm"], 2 * (t - 1))
                    cols = slice(2 * h, 2 * h + 2)
                    nc.vector.tensor_tensor(xgT["lo", s][:, cols].rearrange("p k t -> p (k t)"), S[:, h],
                                            xgT["hi", s][:, cols].rearrange("p k t -> p (k t)"), ALU.subtract
                                            ).then_inc(m["xT_lo_done"], 1)

            def weigh(t, u):
                dve.wait_ge(m["dn_mm"], 2 * t + 2)
                after(dve, m["added"], 16 * SUBS * (t - 1))
                nc.vector.tensor_scalar(y[u % 2][:, 1], T[1][:], lst[u % RING][:].bitcast(F32)[:, 1, 1:2], None,
                                        ALU.mult).then_inc(m["y_dve"], 1)

            weights_lo(dve, 0, 0)
            weights_lo(dve, 1, 1)
            xT_lo(0, 0)
            xT_lo(1, 1)
            weights_lo(dve, 2, 2)

            def tile(t, u, n, left):
                first, second = GU[u % 2]
                for c, dst, src, gate in ((1, mid_a, first[:, TILE:2 * TILE], silu_a),
                                          (2, mid_b, second[MB:2 * MB, 0:TILE], silu_b)):
                    dve.wait_ge(m["silu_done"], 2 * t + c)
                    after(dve, m["mid_lo_done"], 2 * (t - 1) + c)
                    nc.vector.scalar_tensor_tensor(dst[:], src, 1.0 / W_SCALE, gate[:], ALU.mult, ALU.mult
                                                   ).then_inc(m["mid_done"], 1)
                if not (isinstance(t, int) and t == 0):
                    weigh(t - 1, u - 1)
                if left >= 2:
                    xT_lo(t + 2, u % 2)
                for c, lo, hi, src in ((1, ma["lo"][:], ma["hi"][:], mid_a), (2, mb[MB:2 * MB], mb[0:MB], mid_b)):
                    dve.wait_ge(m["mid_hi_done"], 2 * t + c)
                    after(dve, m["dn_mm"], SUBS * t)
                    nc.vector.tensor_tensor(lo, src[:], hi, ALU.subtract).then_inc(m["mid_lo_done"], 1)
                if left >= SPLIT_AHEAD:
                    weights_lo(dve, t + SPLIT_AHEAD, u + SPLIT_AHEAD)

            run_tiles(dve, tile)
            weigh(MOE_TILES - 1, (MOE_TILES - 1) % RING)


def kernel(**inputs):
    import ml_dtypes
    import numpy as np
    import concourse.bacc as bacc
    from concourse.bass_utils import run_bass_kernel_spmd

    a = {k: np.ascontiguousarray(np.asarray(v)) for k, v in inputs.items()}

    def by_rows(w):
        return w.reshape(w.shape[0] // P, P, w.shape[1]).transpose(1, 0, 2)

    w_attn = np.stack([by_rows(a[n].T) for n in ("L0_attn_Wq", "L0_attn_Wk", "L0_attn_Wv", "L0_attn_Wo",
                                                 "L0_xattn_Wq", "L0_xattn_Wout")], axis=1)
    gate, up = a["L0_ffn_gate_proj"], a["L0_ffn_up_proj"]
    gu = np.concatenate([gate[:, :, :P], up[:, :, :P], gate[:, :, P:], up[:, :, P:]], axis=2)
    gu = gu.reshape(EXPERTS, KC, P, 2 * MID).transpose(0, 2, 1, 3).reshape(EXPERTS, P, -1)
    down = a["L0_ffn_down_proj"]
    w_expert = np.concatenate([gu, down[:, :P], np.concatenate([down[:, P:]] * 2, axis=1)], axis=2)
    biases = np.broadcast_to(np.stack([a[n] for n in ("L0_attn_bq", "L0_attn_bk", "L0_attn_bv", "L0_attn_bo")]),
                             (P, 4, D))
    half = HD // 2
    freq = (1.0 / 10000.0 ** (np.arange(half, dtype=np.float32) / np.float32(half))).astype(np.float32)
    ang = np.arange(TOK, dtype=np.float32)[:, None] * freq[None, :]
    cos, sin = np.cos(ang), np.sin(ang)
    rope = np.stack([np.concatenate([cos, cos], 1), np.concatenate([-sin, sin], 1)], axis=1)
    t = np.arange(P)
    causal = np.tile(np.where(t[None, :] > t[:, None], -1e30, 0.0), (1, 4))
    fill = np.zeros((LIST_ROWS, 2), np.uint32)
    fill[:, 0] = TOKENS + np.arange(LIST_ROWS) % DUMP
    arrays = {
        "x": a["x"], "ctxT": a["ctx_512"].transpose(0, 2, 1), "w_attn": w_attn,
        "w_kv": a["L0_xattn_Wkv_expand"].T, "w_gate": by_rows(a["L0_ffn_gate_kernel"]),
        "w_expert": w_expert, "biases": biases,
        "ident": np.eye(P, dtype=np.float32), "identb": np.eye(P).astype(ml_dtypes.bfloat16),
        "rope": rope.astype(np.float32), "causal": causal.astype(ml_dtypes.bfloat16),
        "upper": (t[:, None] < t[None, :]).astype(ml_dtypes.bfloat16),
        "onesb": np.ones((P, P), ml_dtypes.bfloat16),
        "iota_e": np.broadcast_to(np.arange(EXPERTS, dtype=np.float32), (P, EXPERTS)),
        "list_rows0": np.broadcast_to(np.arange(EXPERTS, dtype=np.float32) * TOKENS, (P, EXPERTS)),
        "iota_p": t[:, None].astype(np.float32), "list_fill": fill.reshape(P, -1),
    }
    arrays = {k: np.ascontiguousarray(v) for k, v in arrays.items()}
    nc = bacc.Bacc("TRN2", target_bir_lowering=False, num_devices=1)
    args = [nc.dram_tensor(k, v.shape, mybir.dt.from_np(v.dtype), kind="ExternalInput").ap()
            for k, v in arrays.items()]
    out = nc.dram_tensor("out_rows", (TOKENS + DUMP, D), F32, kind="ExternalOutput").ap()
    build(nc, *args, out)
    r = run_bass_kernel_spmd(nc, [arrays], core_ids=[0])
    return r.results[0]["out_rows"][:TOKENS].reshape(SEQS, TOK, D)
```
